# Optimizing a Trainium2 kernel written in Bass

```python
import numpy as np
import jax
import jax.numpy as jnp

def _softmax(x, axis=-1):
    return jax.nn.softmax(x, axis=axis)

def _gelu(x):
    return jax.nn.gelu(x, approximate=True)

def _silu(x):
    return jax.nn.silu(x)

def _sigmoid(x):
    return jax.nn.sigmoid(x)

def _layernorm(x, axis=-1, eps=1e-05):
    m = jnp.mean(x, axis=axis, keepdims=True)
    v = jnp.var(x, axis=axis, keepdims=True)
    return (x - m) / jnp.sqrt(v + eps)

def _scatter_add(tgt, idx, src, axis=0):
    return tgt.at[idx].add(src)

def _segment_sum(src, seg, n):
    return jax.ops.segment_sum(src, seg, n)
kernel_name = 'mk_macaron_d2_jaxref_r8_2f1d68'

def setup_inputs(seed: int=0):
    np.random.seed(seed)
    _w = jnp.asarray

    def _L0_attn_setup():
        import math
        import jax, jax.numpy as jnp
        import numpy as np
        EMBED_DIM = 128
        ZDIM = 128
        CHUNK = 256
        DSTATE = 16
        DT_RANK = math.ceil(EMBED_DIM / 16)

        def silu(x):
            return x * jax.nn.sigmoid(x)

        def rmsnorm(x, w, eps=1e-05):
            var = jnp.mean(x * x, axis=-1, keepdims=True)
            return x * jax.lax.rsqrt(var + eps) * w

        def _rotary(v, sin, cos):
            x1, x2 = jnp.split(v, 2, axis=-1)
            return jnp.concatenate([x1 * cos - x2 * sin, x2 * cos + x1 * sin], axis=-1)

        def rel_pos_bias(alpha, beta, n):
            half = ZDIM // 2
            freqs = jnp.exp(jnp.arange(half, dtype=jnp.float32) * (-math.log(10000.0) / half))
            ang = jnp.arange(n, dtype=jnp.float32)[:, None] * freqs[None, :]
            sin, cos = (jnp.sin(ang), jnp.cos(ang))
            a = _rotary(jnp.broadcast_to(alpha, (n, ZDIM)), sin, cos)
            b = _rotary(jnp.broadcast_to(beta, (n, ZDIM)), sin, cos)
            return jnp.einsum('mk,nk->mn', a, b)

        def s6(u, xproj_w, dt_w, dt_b, A_log, D_p):
            x_dbl = u @ xproj_w.T
            dt, Bm, Cm = jnp.split(x_dbl, [DT_RANK, DT_RANK + DSTATE], axis=-1)
            dt = jax.nn.softplus(dt @ dt_w.T + dt_b)
            A = -jnp.exp(A_log)

            def step(h, inp):
                dt_t, B_t, C_t, u_t = inp
                dA = jnp.exp(dt_t[..., None] * A)
                h = dA * h + (dt_t * u_t)[..., None] * B_t[:, None, :]
                y = jnp.einsum('bdn,bn->bd', h, C_t)
                return (h, y)
            B, L, D = u.shape
            h0 = jnp.zeros((B, D, DSTATE), u.dtype)
            xs = (dt.transpose(1, 0, 2), Bm.transpose(1, 0, 2), Cm.transpose(1, 0, 2), u.transpose(1, 0, 2))
            _, ys = jax.lax.scan(step, h0, xs)
            return ys.transpose(1, 0, 2) + u * D_p
        key = jax.random.key(seed)
        ks = jax.random.split(key, 12)
        std = 0.02
        B, L, D = (2, 512, EMBED_DIM)
        f32 = jnp.float32
        inp = {'x': jax.random.normal(ks[0], (B, L, D), f32), 'norm_w': jnp.ones((D,), f32), 'v_w': jax.random.normal(ks[1], (D, D), f32) * std, 'v_b': jnp.zeros((D,), f32), 'mx_w': jax.random.normal(ks[2], (ZDIM + D + 2 * D, D), f32) * std, 'mx_b': jnp.zeros((ZDIM + 3 * D,), f32), 'h_w': jax.random.normal(ks[3], (D, D), f32) * std, 'h_b': jnp.zeros((D,), f32), 'gamma': jax.random.normal(ks[4], (2, ZDIM), f32) * std, 'beta': jnp.zeros((2, ZDIM), f32), 'alpha_rb': jax.random.normal(ks[5], (1, ZDIM), f32) * std, 'beta_rb': jax.random.normal(ks[6], (1, ZDIM), f32) * std, 'xproj_w': jax.random.normal(ks[7], (DT_RANK + 2 * DSTATE, D), f32) * std, 'dt_w': jax.random.normal(ks[8], (D, DT_RANK), f32) * std, 'dt_b': jnp.full((D,), -4.6, f32), 'A_log': jnp.log(jnp.broadcast_to(jnp.arange(1, DSTATE + 1, dtype=f32), (D, DSTATE))), 'D_p': jnp.ones((D,), f32)}
        return inp
    _L0_attn_in = _L0_attn_setup()

    def _L0_ffn_setup():
        import jax, jax.numpy as jnp
        import numpy as np
        TOP_K = 2
        NUM_EXPERTS = 8
        key = jax.random.key(seed)
        ks = jax.random.split(key, 8)
        h, d, ds, E = (128, 64, 128, NUM_EXPERTS)
        s = 1.0 / np.sqrt(h)
        return {'x': jax.random.normal(ks[0], (2, 256, h), jnp.float32), 'router': jax.random.normal(ks[1], (h, E), jnp.float32) * s, 'experts_gate': jax.random.normal(ks[2], (E, h, d), jnp.float32) * s, 'experts_up': jax.random.normal(ks[3], (E, h, d), jnp.float32) * s, 'experts_down': jax.random.normal(ks[4], (E, d, h), jnp.float32) * (1.0 / np.sqrt(d)), 'shared_gate': jax.random.normal(ks[5], (h, ds), jnp.float32) * s, 'shared_up': jax.random.normal(ks[6], (h, ds), jnp.float32) * s, 'shared_down': jax.random.normal(ks[7], (ds, h), jnp.float32) * (1.0 / np.sqrt(ds))}
    _L0_ffn_in = _L0_ffn_setup()

    def _L1_attn_setup():
        import jax, jax.numpy as jnp
        import numpy as np
        import math
        B, N, D = (64, 64, 128)
        SHELL_DIM, RFF_DIM, ORDER = (64, 32, 4)
        CHARGE_COUPLING, SHELL_COUPLING = (1.0, 0.5)
        DIST_COUPLING, DIST_SCALE = (0.3, 10.0)
        COMBINED_DIM = 64

        def _forward(x, W_charge, b_charge, W_shell, b_shell, omega, rff_bias, W_combine, W_v, b_v, W_out, b_out, log_temp):
            b, n, d = x.shape
            q = jnp.tanh(x @ W_charge.T + b_charge)[..., 0]
            coeffs = jnp.asarray([(-CHARGE_COUPLING) ** m / math.factorial(m) for m in range(ORDER + 1)], dtype=x.dtype)
            mags = jnp.sqrt(jnp.abs(coeffs) + 1e-10)
            phi_c = mags * q[..., None] ** jnp.arange(ORDER + 1)
            shell = x @ W_shell.T + b_shell
            shell = shell / jnp.maximum(jnp.linalg.norm(shell, axis=-1, keepdims=True), 1e-12)
            proj = shell @ omega.T + rff_bias
            rff_scale = math.sqrt(2.0 / (2 * RFF_DIM)) * math.sqrt(math.exp(-SHELL_COUPLING))
            phi_s = jnp.concatenate([jnp.cos(proj), jnp.sin(proj)], axis=-1) * rff_scale
            tp = (phi_c[..., :, None] * phi_s[..., None, :]).reshape(b, n, -1)
            phi = tp @ W_combine.T
            idx = jnp.arange(n)
            T = jnp.exp(-DIST_COUPLING * jnp.abs(idx[:, None] - idx[None, :]).astype(x.dtype) / DIST_SCALE)
            temp = jax.nn.softplus(log_temp) + 0.1
            logits = jnp.einsum('bnd,bmd->bnm', phi, phi) * T / temp
            causal = idx[:, None] >= idx[None, :]
            logits = jnp.where(causal, logits, -jnp.inf)
            attn = jax.nn.softmax(logits, axis=-1)
            V = x @ W_v.T + b_v
            out = jnp.einsum('bnm,bmd->bnd', attn, V)
            return out @ W_out.T + b_out
        key = jax.random.key(seed)
        ks = jax.random.split(key, 12)
        s = 0.02
        inp = {'x': jax.random.normal(ks[0], (B, N, D), dtype=jnp.float32), 'W_charge': jax.random.normal(ks[1], (1, D), dtype=jnp.float32) * s, 'b_charge': jnp.zeros((1,), dtype=jnp.float32), 'W_shell': jax.random.normal(ks[2], (SHELL_DIM, D), dtype=jnp.float32) * s, 'b_shell': jnp.zeros((SHELL_DIM,), dtype=jnp.float32), 'omega': jax.random.normal(ks[3], (RFF_DIM, SHELL_DIM), dtype=jnp.float32) * math.sqrt(SHELL_COUPLING), 'rff_bias': jax.random.uniform(ks[4], (RFF_DIM,), dtype=jnp.float32) * (2.0 * math.pi), 'W_combine': jax.random.normal(ks[5], (COMBINED_DIM, (ORDER + 1) * 2 * RFF_DIM), dtype=jnp.float32) * s, 'W_v': jax.random.normal(ks[6], (D, D), dtype=jnp.float32) * s, 'b_v': jnp.zeros((D,), dtype=jnp.float32), 'W_out': jax.random.normal(ks[7], (D, D), dtype=jnp.float32) * s, 'b_out': jnp.zeros((D,), dtype=jnp.float32), 'log_temp': jnp.zeros((), dtype=jnp.float32)}
        return inp
    _L1_attn_in = _L1_attn_setup()

    def _L1_ffn_setup():
        import jax, jax.numpy as jnp
        import numpy as np
        B, L, D, F, E = (2, 128, 128, 512, 8)
        key = jax.random.key(seed)
        ks = jax.random.split(key, 7)
        return {'x': jax.random.normal(ks[0], (B, L, D), dtype=jnp.float32), 'router_w': jax.random.normal(ks[1], (D, E), dtype=jnp.float32) * 0.02, 'router_b': jax.random.normal(ks[2], (E,), dtype=jnp.float32) * 0.02, 'W1': jax.random.normal(ks[3], (E, D, F), dtype=jnp.float32) * (1.0 / np.sqrt(D)), 'b1': jax.random.normal(ks[4], (E, F), dtype=jnp.float32) * 0.02, 'W2': jax.random.normal(ks[5], (E, F, D), dtype=jnp.float32) * (1.0 / np.sqrt(F)), 'b2': jax.random.normal(ks[6], (E, D), dtype=jnp.float32) * 0.02}
    _L1_ffn_in = _L1_ffn_setup()
    _d = {'L0_attn_x': _L0_attn_in['x'], 'L0_attn_norm_w': _L0_attn_in['norm_w'], 'L0_attn_v_w': _L0_attn_in['v_w'], 'L0_attn_v_b': _L0_attn_in['v_b'], 'L0_attn_mx_w': _L0_attn_in['mx_w'], 'L0_attn_mx_b': _L0_attn_in['mx_b'], 'L0_attn_h_w': _L0_attn_in['h_w'], 'L0_attn_h_b': _L0_attn_in['h_b'], 'L0_attn_gamma': _L0_attn_in['gamma'], 'L0_attn_beta': _L0_attn_in['beta'], 'L0_attn_alpha_rb': _L0_attn_in['alpha_rb'], 'L0_attn_beta_rb': _L0_attn_in['beta_rb'], 'L0_attn_xproj_w': _L0_attn_in['xproj_w'], 'L0_attn_dt_w': _L0_attn_in['dt_w'], 'L0_attn_dt_b': _L0_attn_in['dt_b'], 'L0_attn_A_log': _L0_attn_in['A_log'], 'L0_attn_D_p': _L0_attn_in['D_p'], 'L0_ffn_router': _L0_ffn_in['router'], 'L0_ffn_experts_gate': _L0_ffn_in['experts_gate'], 'L0_ffn_experts_up': _L0_ffn_in['experts_up'], 'L0_ffn_experts_down': _L0_ffn_in['experts_down'], 'L0_ffn_shared_gate': _L0_ffn_in['shared_gate'], 'L0_ffn_shared_up': _L0_ffn_in['shared_up'], 'L0_ffn_shared_down': _L0_ffn_in['shared_down'], 'L1_attn_W_charge': _L1_attn_in['W_charge'], 'L1_attn_b_charge': _L1_attn_in['b_charge'], 'L1_attn_W_shell': _L1_attn_in['W_shell'], 'L1_attn_b_shell': _L1_attn_in['b_shell'], 'L1_attn_omega': _L1_attn_in['omega'], 'L1_attn_rff_bias': _L1_attn_in['rff_bias'], 'L1_attn_W_combine': _L1_attn_in['W_combine'], 'L1_attn_W_v': _L1_attn_in['W_v'], 'L1_attn_b_v': _L1_attn_in['b_v'], 'L1_attn_W_out': _L1_attn_in['W_out'], 'L1_attn_b_out': _L1_attn_in['b_out'], 'L1_attn_log_temp': _L1_attn_in['log_temp'], 'L1_ffn_router_w': _L1_ffn_in['router_w'], 'L1_ffn_router_b': _L1_ffn_in['router_b'], 'L1_ffn_W1': _L1_ffn_in['W1'], 'L1_ffn_b1': _L1_ffn_in['b1'], 'L1_ffn_W2': _L1_ffn_in['W2'], 'L1_ffn_b2': _L1_ffn_in['b2']}
    _x0 = _d['L0_attn_x']
    _d['L0_attn_x'] = jax.random.normal(jax.random.fold_in(jax.random.key(seed), 1), (8, 1024, 128), dtype=_x0.dtype)
    del _x0
    return _d

def reference(L0_attn_x, L0_attn_norm_w, L0_attn_v_w, L0_attn_v_b, L0_attn_mx_w, L0_attn_mx_b, L0_attn_h_w, L0_attn_h_b, L0_attn_gamma, L0_attn_beta, L0_attn_alpha_rb, L0_attn_beta_rb, L0_attn_xproj_w, L0_attn_dt_w, L0_attn_dt_b, L0_attn_A_log, L0_attn_D_p, L0_ffn_router, L0_ffn_experts_gate, L0_ffn_experts_up, L0_ffn_experts_down, L0_ffn_shared_gate, L0_ffn_shared_up, L0_ffn_shared_down, L1_attn_W_charge, L1_attn_b_charge, L1_attn_W_shell, L1_attn_b_shell, L1_attn_omega, L1_attn_rff_bias, L1_attn_W_combine, L1_attn_W_v, L1_attn_b_v, L1_attn_W_out, L1_attn_b_out, L1_attn_log_temp, L1_ffn_router_w, L1_ffn_router_b, L1_ffn_W1, L1_ffn_b1, L1_ffn_W2, L1_ffn_b2):

    def _L0_attn_ref(x, norm_w, v_w, v_b, mx_w, mx_b, h_w, h_b, gamma, beta, alpha_rb, beta_rb, xproj_w, dt_w, dt_b, A_log, D_p):
        import math
        import jax, jax.numpy as jnp
        import numpy as np
        EMBED_DIM = 128
        ZDIM = 128
        CHUNK = 256
        DSTATE = 16
        DT_RANK = math.ceil(EMBED_DIM / 16)

        def silu(x):
            return x * jax.nn.sigmoid(x)

        def rmsnorm(x, w, eps=1e-05):
            var = jnp.mean(x * x, axis=-1, keepdims=True)
            return x * jax.lax.rsqrt(var + eps) * w

        def _rotary(v, sin, cos):
            x1, x2 = jnp.split(v, 2, axis=-1)
            return jnp.concatenate([x1 * cos - x2 * sin, x2 * cos + x1 * sin], axis=-1)

        def rel_pos_bias(alpha, beta, n):
            half = ZDIM // 2
            freqs = jnp.exp(jnp.arange(half, dtype=jnp.float32) * (-math.log(10000.0) / half))
            ang = jnp.arange(n, dtype=jnp.float32)[:, None] * freqs[None, :]
            sin, cos = (jnp.sin(ang), jnp.cos(ang))
            a = _rotary(jnp.broadcast_to(alpha, (n, ZDIM)), sin, cos)
            b = _rotary(jnp.broadcast_to(beta, (n, ZDIM)), sin, cos)
            return jnp.einsum('mk,nk->mn', a, b)

        def s6(u, xproj_w, dt_w, dt_b, A_log, D_p):
            x_dbl = u @ xproj_w.T
            dt, Bm, Cm = jnp.split(x_dbl, [DT_RANK, DT_RANK + DSTATE], axis=-1)
            dt = jax.nn.softplus(dt @ dt_w.T + dt_b)
            A = -jnp.exp(A_log)

            def step(h, inp):
                dt_t, B_t, C_t, u_t = inp
                dA = jnp.exp(dt_t[..., None] * A)
                h = dA * h + (dt_t * u_t)[..., None] * B_t[:, None, :]
                y = jnp.einsum('bdn,bn->bd', h, C_t)
                return (h, y)
            B, L, D = u.shape
            h0 = jnp.zeros((B, D, DSTATE), u.dtype)
            xs = (dt.transpose(1, 0, 2), Bm.transpose(1, 0, 2), Cm.transpose(1, 0, 2), u.transpose(1, 0, 2))
            _, ys = jax.lax.scan(step, h0, xs)
            return ys.transpose(1, 0, 2) + u * D_p
        B, L, D = x.shape
        residual = x
        xn = rmsnorm(x, norm_w)
        v = silu(xn @ v_w.T + v_b)
        mx = silu(s6(xn, xproj_w, dt_w, dt_b, A_log, D_p))
        base = mx @ mx_w.T + mx_b
        u, zr, hx = jnp.split(base, [D, D + ZDIM + D], axis=-1)
        u = jax.nn.sigmoid(u)
        zr = silu(zr)
        z, r = jnp.split(zr, [ZDIM], axis=-1)
        z = z[..., None, :] * gamma + beta
        q, k = (z[..., 0, :], z[..., 1, :])
        c = min(CHUNK, L)
        nc = L // c
        qh = q.reshape(B, nc, c, ZDIM) * ZDIM ** (-0.5)
        kh = k.reshape(B, nc, c, ZDIM)
        vh = v.reshape(B, nc, c, D)
        bias = rel_pos_bias(alpha_rb, beta_rb, c)
        mask = jnp.triu(jnp.full((c, c), -jnp.inf, jnp.float32), 1)
        qk = jnp.einsum('bnqz,bnkz->bnqk', qh, kh) + bias + mask
        attn = jax.nn.softmax(qk.astype(jnp.float32), axis=-1).astype(qk.dtype)
        h = jnp.einsum('bnqk,bnkd->bnqd', attn, vh).reshape(B, L, D)
        h = silu(hx + h * r @ h_w.T + h_b)
        return residual + u * (h - residual)

    def _L0_ffn_ref(x, router, experts_gate, experts_up, experts_down, shared_gate, shared_up, shared_down):
        import jax, jax.numpy as jnp
        import numpy as np
        TOP_K = 2
        NUM_EXPERTS = 8
        b, s, h = x.shape
        E = router.shape[1]
        shared_act = jax.nn.silu(jnp.einsum('bsh,hd->bsd', x, shared_gate))
        shared_up_out = jnp.einsum('bsh,hd->bsd', x, shared_up)
        shared_out = jnp.einsum('bsd,dh->bsh', shared_act * shared_up_out, shared_down)
        router_probs = jax.nn.softmax(jnp.einsum('bsh,he->bse', x, router), axis=-1)
        topk_probs, topk_idx = jax.lax.top_k(router_probs, TOP_K)
        coef = jnp.sum(jax.nn.one_hot(topk_idx, E, dtype=x.dtype) * topk_probs[..., None], axis=2)
        coef = coef.reshape(b * s, E)
        x_flat = x.reshape(b * s, h)
        gate = jnp.einsum('th,ehd->etd', x_flat, experts_gate)
        up = jnp.einsum('th,ehd->etd', x_flat, experts_up)
        expert_out = jnp.einsum('etd,edh->eth', jax.nn.silu(gate) * up, experts_down)
        routed = jnp.einsum('eth,te->th', expert_out, coef)
        return routed.reshape(b, s, h) + shared_out

    def _L1_attn_ref(x, W_charge, b_charge, W_shell, b_shell, omega, rff_bias, W_combine, W_v, b_v, W_out, b_out, log_temp):
        import jax, jax.numpy as jnp
        import numpy as np
        import math
        B, N, D = (64, 64, 128)
        SHELL_DIM, RFF_DIM, ORDER = (64, 32, 4)
        CHARGE_COUPLING, SHELL_COUPLING = (1.0, 0.5)
        DIST_COUPLING, DIST_SCALE = (0.3, 10.0)
        COMBINED_DIM = 64

        def _forward(x, W_charge, b_charge, W_shell, b_shell, omega, rff_bias, W_combine, W_v, b_v, W_out, b_out, log_temp):
            b, n, d = x.shape
            q = jnp.tanh(x @ W_charge.T + b_charge)[..., 0]
            coeffs = jnp.asarray([(-CHARGE_COUPLING) ** m / math.factorial(m) for m in range(ORDER + 1)], dtype=x.dtype)
            mags = jnp.sqrt(jnp.abs(coeffs) + 1e-10)
            phi_c = mags * q[..., None] ** jnp.arange(ORDER + 1)
            shell = x @ W_shell.T + b_shell
            shell = shell / jnp.maximum(jnp.linalg.norm(shell, axis=-1, keepdims=True), 1e-12)
            proj = shell @ omega.T + rff_bias
            rff_scale = math.sqrt(2.0 / (2 * RFF_DIM)) * math.sqrt(math.exp(-SHELL_COUPLING))
            phi_s = jnp.concatenate([jnp.cos(proj), jnp.sin(proj)], axis=-1) * rff_scale
            tp = (phi_c[..., :, None] * phi_s[..., None, :]).reshape(b, n, -1)
            phi = tp @ W_combine.T
            idx = jnp.arange(n)
            T = jnp.exp(-DIST_COUPLING * jnp.abs(idx[:, None] - idx[None, :]).astype(x.dtype) / DIST_SCALE)
            temp = jax.nn.softplus(log_temp) + 0.1
            logits = jnp.einsum('bnd,bmd->bnm', phi, phi) * T / temp
            causal = idx[:, None] >= idx[None, :]
            logits = jnp.where(causal, logits, -jnp.inf)
            attn = jax.nn.softmax(logits, axis=-1)
            V = x @ W_v.T + b_v
            out = jnp.einsum('bnm,bmd->bnd', attn, V)
            return out @ W_out.T + b_out
        return _forward(x, W_charge, b_charge, W_shell, b_shell, omega, rff_bias, W_combine, W_v, b_v, W_out, b_out, log_temp)

    def _L1_ffn_ref(x, router_w, router_b, W1, b1, W2, b2):
        import jax, jax.numpy as jnp
        import numpy as np
        B, L, D, F, E = (2, 128, 128, 512, 8)
        b, l, d = x.shape
        xf = x.reshape(b * l, d)
        logits = xf @ router_w + router_b
        top1 = jnp.argmax(logits, axis=-1)
        h = jax.nn.gelu(jnp.einsum('td,edf->etf', xf, W1) + b1[:, None, :], approximate=False)
        y_all = jnp.einsum('etf,efd->etd', h, W2) + b2[:, None, :]
        onehot = jax.nn.one_hot(top1, E, dtype=x.dtype)
        yf = jnp.einsum('te,etd->td', onehot, y_all)
        return yf.reshape(b, l, d)
    x = L0_attn_x
    x = x + 0.5 * _L0_ffn_ref(_layernorm(x, axis=-1), L0_ffn_router, L0_ffn_experts_gate, L0_ffn_experts_up, L0_ffn_experts_down, L0_ffn_shared_gate, L0_ffn_shared_up, L0_ffn_shared_down)
    x = x + _L0_attn_ref(_layernorm(x, axis=-1), L0_attn_norm_w, L0_attn_v_w, L0_attn_v_b, L0_attn_mx_w, L0_attn_mx_b, L0_attn_h_w, L0_attn_h_b, L0_attn_gamma, L0_attn_beta, L0_attn_alpha_rb, L0_attn_beta_rb, L0_attn_xproj_w, L0_attn_dt_w, L0_attn_dt_b, L0_attn_A_log, L0_attn_D_p)
    x = x + 0.5 * _L0_ffn_ref(_layernorm(x, axis=-1), L0_ffn_router, L0_ffn_experts_gate, L0_ffn_experts_up, L0_ffn_experts_down, L0_ffn_shared_gate, L0_ffn_shared_up, L0_ffn_shared_down)
    x = x + 0.5 * _L1_ffn_ref(_layernorm(x, axis=-1), L1_ffn_router_w, L1_ffn_router_b, L1_ffn_W1, L1_ffn_b1, L1_ffn_W2, L1_ffn_b2)
    x = x + _L1_attn_ref(_layernorm(x, axis=-1), L1_attn_W_charge, L1_attn_b_charge, L1_attn_W_shell, L1_attn_b_shell, L1_attn_omega, L1_attn_rff_bias, L1_attn_W_combine, L1_attn_W_v, L1_attn_b_v, L1_attn_W_out, L1_attn_b_out, L1_attn_log_temp)
    x = x + 0.5 * _L1_ffn_ref(_layernorm(x, axis=-1), L1_ffn_router_w, L1_ffn_router_b, L1_ffn_W1, L1_ffn_b1, L1_ffn_W2, L1_ffn_b2)
    return x

_drawn_inputs = setup_inputs


def setup_inputs(seed=0):
    import zlib

    import numpy as np

    out = dict(_drawn_inputs(seed))
    spreads = {'L0_attn_norm_w': (1.0, 0.2),
     'L0_attn_v_b': (0.0, 0.8),
     'L0_attn_mx_b': (0.0, 0.1),
     'L0_attn_h_b': (0.0, 0.1),
     'L0_attn_beta': (0.0, 2.0),
     'L0_attn_dt_b': (-4.599999904632568, 0.6),
     'L0_attn_D_p': (1.0, 0.2),
     'L1_attn_b_shell': (0.0, 2.0),
     'L1_attn_b_v': (0.0, 0.272),
     'L1_attn_b_out': (0.0, 0.1)}
    factors = {'L0_attn_v_w': 8.0,
     'L0_attn_h_w': 8.0,
     'L0_attn_gamma': 64.0,
     'L0_attn_alpha_rb': 33.667,
     'L0_attn_beta_rb': 40.619,
     'L0_attn_xproj_w': 8.0,
     'L0_attn_dt_w': 8.0,
     'L0_attn_A_log': 8.0,
     'L1_attn_W_charge': 200.0,
     'L1_attn_W_shell': 200.0,
     'L1_attn_omega': 200.0,
     'L1_attn_rff_bias': 200.0,
     'L1_attn_W_combine': 200.0,
     'L1_attn_W_v': 5.18,
     'L1_ffn_b1': 3.439,
     'L1_ffn_b2': 2.7}
    for name, (base, spread) in spreads.items():
        noise = np.random.default_rng([zlib.crc32(name.encode()), seed]).standard_normal(out[name].shape)
        drawn = base * np.exp(spread * noise) if base else spread * noise
        out[name] = jnp.asarray(drawn.astype(out[name].dtype))
    for name, factor in factors.items():
        out[name] = (out[name] * factor).astype(out[name].dtype)
    return out
```

```python
from contextlib import ExitStack

import concourse.bass as bass
import numpy as np
from concourse import mybir

ALU = mybir.AluOpType
ACT = mybir.ActivationFunctionType
AX = mybir.AxisListType
F32 = mybir.dt.float32
BF16 = mybir.dt.bfloat16
I32 = mybir.dt.int32

P = 128
D = 128
BLOCK = 512
TB = BLOCK // P
EPS = 1e-5
BIG = 1e30


class Core:

    def __init__(self, nc, ctx, tokens):
        self.nc, self.ctx = nc, ctx
        self.tokens = tokens
        self.used = []
        self.tiles = tokens // P
        self.blocks = tokens // BLOCK
        self.X = self.sb("X", [P, self.tiles, D])
        self.stats = self.sb("stats", [P, self.tiles, 6])
        self.rstd = self.sb("rstd", [P, self.tiles])
        self.shift = self.sb("shift", [P, self.tiles])
        self.ln_tmp = self.sb("ln_tmp", [P, 4, self.tiles])
        self.eps = self.sb("eps", [P, 1])
        self.ident = self.sb("ident", [P, P])
        self.ident_bf = self.sb("ident_bf", [P, P], BF16)
        self.ps = ctx.enter_context(nc.psum_tensor("ps", [P, 8, BLOCK], F32))

    def sb(self, name, shape, dt=F32, ctx=None):
        return (ctx or self.ctx).enter_context(self.nc.sbuf_tensor(name, shape, dt))

    def sems(self, ctx, stage, names):
        made = [ctx.enter_context(self.nc.semaphore(f"{stage}_{n}")) for n in names.split()]
        self.used += [s.num for s in made]
        return made

    def clear_semaphores(self):
        used, self.used = sorted(set(self.used)), []
        with self.nc.Block() as block:
            @block.gpsimd
            def _(pool):
                while used:
                    n = 1
                    while n < len(used) and used[n] == used[0] + n:
                        n += 1
                    pool.sem_clear(range(used[0], used[0] + n))
                    del used[:n]


def chained(engine, sem):
    count = [0]

    def step(instruction):
        count[0] += 1
        instruction.then_inc(sem, 1)
        engine.wait_ge(sem, count[0])
        return count[0]
    return step


def ln_scale_dve(k, dve, step, std_ready, var_ready):
    me, mo = k.stats[:, :, 1], k.stats[:, :, 4]
    qe, qo = k.stats[:, :, 2], k.stats[:, :, 5]
    msum, var, a, b = (k.ln_tmp[:, n, :] for n in range(4))
    step(dve.tensor_tensor(a, me, mo, ALU.subtract))
    step(dve.tensor_tensor(b, a, a, ALU.mult))
    step(dve.tensor_tensor(a, qe, qo, ALU.add))
    step(dve.tensor_scalar(a, a, 1.0 / D, EPS, ALU.mult, ALU.add))
    dve.scalar_tensor_tensor(out=var, in0=b, scalar=0.25, in1=a, op0=ALU.mult, op1=ALU.add).then_inc(var_ready, 1)
    step(dve.tensor_tensor(msum, me, mo, ALU.add))
    dve.wait_ge(std_ready, 1)
    step(dve.reciprocal(k.rstd[:], b))
    step(dve.tensor_tensor(a, k.rstd[:], k.rstd[:], ALU.mult))
    step(dve.tensor_tensor(a, a, var, ALU.mult))
    step(dve.tensor_scalar(a, a, -0.5, 1.5, ALU.mult, ALU.add))
    step(dve.tensor_tensor(k.rstd[:], k.rstd[:], a, ALU.mult))
    step(dve.scalar_tensor_tensor(out=k.shift[:], in0=msum, scalar=-0.5, in1=k.rstd[:], op0=ALU.mult, op1=ALU.mult))


def ln_scale_act(k, act, var_ready, std_ready):
    act.wait_ge(var_ready, 1)
    act.activation(k.ln_tmp[:, 3, :], k.ln_tmp[:, 1, :], ACT.Sqrt).then_inc(std_ready, 1)


def normalised(k, dve, out, tile):
    return dve.tensor_scalar(out, k.X[:, bass.ds(tile, 1), :].rearrange("p a f -> p (a f)"),
                             k.rstd[:, bass.ds(tile, 1)], k.shift[:, bass.ds(tile, 1)], ALU.mult, ALU.add)


def normalise_block(k, dve, out, i, scaled, done, count):
    per_token = lambda a: a[:, bass.ds(i * TB, TB)].rearrange("p (t a) -> p t a", a=1).broadcast_to([P, TB, D])
    dve.tensor_tensor(out, k.X[:, bass.ds(i * TB, TB), :], per_token(k.rstd), ALU.mult).then_inc(scaled, 1)
    dve.wait_ge(scaled, count + 1)
    dve.tensor_tensor(out, out, per_token(k.shift), ALU.add).then_inc(done, 1)


def tile_stats(k, dve, tile):
    return dve.bn_stats(k.stats[:, bass.ds(tile, 1), :].rearrange("p a s -> p (a s)"),
                        k.X[:, bass.ds(tile, 1), :].rearrange("p a f -> p (a f)"))


def stage_load(k, x, ident_dram):
    nc = k.nc
    parts = 4
    n = k.tiles // parts
    with ExitStack() as ctx:
        loaded = k.sems(ctx, "load", " ".join(f"x{c}" for c in range(parts)))
        consts, stats_done = k.sems(ctx, "load", "consts stats_done")
        with nc.Block() as block:
            @block.sync
            def _(sp):
                view = x.rearrange("(t p) f -> p t f", p=P)
                for c in range(parts):
                    sp.dma_start(k.X[:, c * n:(c + 1) * n, :], view[:, c * n:(c + 1) * n, :]).then_inc(loaded[c], 16)

            @block.scalar
            def _(act):
                act.dma_start(k.ident[:], ident_dram).then_inc(consts, 16)
                act.wait_ge(consts, 16)
                act.activation(k.ident_bf[:], k.ident[:], ACT.Copy)

            @block.vector
            def _(dve):
                dve.memset(k.eps[:], EPS)
                for c in range(parts):
                    dve.wait_ge(loaded[c], 16)
                    for t in range(c * n, (c + 1) * n):
                        dve.bn_stats(k.stats[:, t, :], k.X[:, t, :]).then_inc(stats_done, 1)


def stage_store(k, out):
    nc = k.nc
    with ExitStack() as ctx:
        stored, = k.sems(ctx, "store", "stored")
        with nc.Block() as block:
            @block.sync
            def _(sp):
                sp.dma_start(out.rearrange("(t p) f -> p t f", p=P), k.X[:]).then_inc(stored, 16)
                sp.wait_ge(stored, 16)


def stage_ffn0(k, name, w):
    nc = k.nc
    E, H = 8, 64
    NJ = E * H // P + 1
    NBLK = k.blocks
    G = 4
    GT = G * TB
    LEAD = 5
    with ExitStack() as ctx:
        sb = lambda n, shape, dt=F32: k.sb(f"{name}_{n}", shape, dt, ctx)
        wg, wu, wd = sb("wg", [P, NJ * P]), sb("wu", [P, NJ * P]), sb("wd", [P, NJ, D])
        router = sb("router", [P, E])
        sel = sb("sel", [P, TB * (NJ - 1), P], BF16)
        xt = sb("xt", [P, k.tokens])
        xn, xtp = sb("xn", [P, 2, TB, D]), sb("xtp", [P, BLOCK])
        lg, ex, oh, tmp = (sb(n, [P, GT, E]) for n in ("lg", "ex", "oh", "tmp"))
        em8 = sb("em8", [P, GT, E])
        m1 = sb("m1", [P, GT])
        parts = sb("parts", [P, GT, 32], BF16)
        coef_t = sb("coef_t", [P, NBLK * P], BF16)
        silu = sb("silu", [P, 2, BLOCK])
        prod = sb("prod", [P, 2, BLOCK])
        hid = sb("hid", [P, 2, NJ, BLOCK])
        ps = k.ps
        DOWN, SHARED = 6, 7
        (w_in, w_dn, w_rt, var_ready, std_ready, dve_step, xn_scaled, xn_ready, turned, xt_kept, lg_done, lg_kept, ex_in, ex_done,
         routed, parts_ready, coef_ps, coef_sb, gated, siluq, prodded, scaled, coefd, down, resid, stats_done) = k.sems(
            ctx, name, "w_in w_dn w_rt var_ready std_ready dve_step xn_scaled xn_ready turned xt_kept lg_done lg_kept ex_in ex_done "
            "routed parts_ready coef_ps coef_sb gated siluq prodded scaled coefd down resid stats_done")

        def steps(engine, step):
            with engine.Fori(0, NBLK // G - 2) as g:
                for r in range(G):
                    step(g * G + r, g, r, True, r == 1, r == 2, True)
            for g in (NBLK // G - 2, NBLK // G - 1):
                for r in range(G):
                    s, routes = g * G + r, g == NBLK // G - 2
                    step(s, g, r, s + 1 + LEAD < NBLK, routes and r == 1, routes and r == 2, s + 1 < NBLK)

        with nc.Block() as block:
            @block.sync
            def _(sp):
                sp.dma_start(router[:], w["router"]).then_inc(w_rt, 16)
                sp.dma_start(em8[:].rearrange("p t e -> p (t e)"), w["em8"][:, 0:GT * E]).then_inc(w_rt, 16)
                sp.dma_start(wg[:, 0:E * H].rearrange("p (e d) -> p e d", d=H), w["eg"].rearrange("e h d -> h e d")).then_inc(w_in, 16)
                sp.dma_start(wu[:, 0:E * H].rearrange("p (e d) -> p e d", d=H), w["eu"].rearrange("e h d -> h e d")).then_inc(w_in, 16)
                sp.dma_start(wg[:, E * H:], w["sg"]).then_inc(w_in, 16)
                sp.dma_start(wu[:, E * H:], w["su"]).then_inc(w_in, 16)
                sp.dma_start(sel[:], w["sel"].rearrange("p (a b) -> p a b", b=P)).then_inc(w_in, 16)
                sp.dma_start(wd[:, 0:NJ - 1, :], w["ed"].rearrange("e d h -> (e d) h").rearrange("(c p) n -> p c n", p=P)).then_inc(w_dn, 16)
                sp.dma_start(wd[:, NJ - 1, :], w["sd"]).then_inc(w_dn, 16)
                sp.wait_ge(w_dn, 32)

            @block.vector
            def _(dve):
                chain = chained(dve, dve_step)
                ln_scale_dve(k, dve, chain, std_ready, var_ready)
                for credit, n in ((xn_ready, 1), (prodded, 2), (scaled, 2), (resid, 1), (lg_kept, 1)):
                    dve.sem_inc(credit, n)
                bc = lambda a: a.rearrange("p (t a) -> p t a", a=1).broadcast_to([P, GT, E])

                def normalise(m, v):
                    dve.wait_ge(turned, m + 1)
                    normalise_block(k, dve, xn[:, v, :, :], m, xn_scaled, xn_ready, m)

                def keep_logits(m, slot):
                    dve.wait_ge(lg_done, m + 1)
                    dve.tensor_copy(lg[:, slot * TB:(slot + 1) * TB, :], ps[:, SHARED, 0:TB * E].rearrange("p (t e) -> p t e", e=E)).then_inc(lg_kept, 1)

                def routing(g):
                    count = [0]

                    def one(instruction):
                        count[0] += 1
                        instruction.then_inc(routed, 1)
                        dve.wait_ge(routed, g * STEPS + count[0])

                    dve.wait_ge(lg_kept, (g + 1) * G + 1)
                    dve.wait_ge(coef_ps, g + 1)
                    one(dve.tensor_reduce(m1[:], lg[:], AX.X, ALU.max))
                    dve.tensor_tensor(ex[:], lg[:], bc(m1[:]), ALU.subtract).then_inc(ex_in, 1)
                    one(dve.tensor_tensor(tmp[:], lg[:], bc(m1[:]), ALU.is_equal))
                    one(dve.tensor_tensor(tmp[:], tmp[:], em8[:], ALU.mult))
                    one(dve.tensor_reduce(m1[:], tmp[:], AX.X, ALU.min))
                    one(dve.tensor_tensor(oh[:], em8[:], bc(m1[:]), ALU.is_equal))
                    one(dve.scalar_tensor_tensor(out=lg[:], in0=oh[:], scalar=-BIG, in1=lg[:], op0=ALU.mult, op1=ALU.add))
                    one(dve.tensor_reduce(m1[:], lg[:], AX.X, ALU.max))
                    one(dve.tensor_tensor(tmp[:], lg[:], bc(m1[:]), ALU.is_equal))
                    one(dve.tensor_tensor(tmp[:], tmp[:], em8[:], ALU.mult))
                    one(dve.tensor_reduce(m1[:], tmp[:], AX.X, ALU.min))
                    one(dve.tensor_tensor(tmp[:], em8[:], bc(m1[:]), ALU.is_equal))
                    one(dve.tensor_tensor(oh[:], oh[:], tmp[:], ALU.add))
                    dve.wait_ge(ex_done, g + 1)
                    one(dve.tensor_reduce(m1[:], ex[:], AX.X, ALU.add))
                    one(dve.reciprocal(m1[:], m1[:]))
                    one(dve.tensor_tensor(oh[:], oh[:], ex[:], ALU.mult))
                    one(dve.tensor_tensor(oh[:], oh[:], bc(m1[:]), ALU.mult))
                    for c in range(3):
                        part = parts[:, :, c * E:(c + 1) * E]
                        one(dve.tensor_copy(part, oh[:]))
                        if c < 2:
                            one(dve.tensor_tensor(oh[:], oh[:], part, ALU.subtract))
                    dve.sem_inc(parts_ready, 1)
                    assert count[0] == STEPS

                STEPS = 21

                def products(i, u, m, slot):
                    dve.wait_ge(down, i + 1)
                    for j in range(NJ):
                        b = (u + j) % 2
                        dve.wait_ge(siluq, i * NJ + j + 1)
                        last = j == NJ - 1
                        dve.tensor_tensor(hid[:, u, j, :] if last else prod[:, j % 2, :], silu[:, b, :], ps[:, 2 + b, :],
                                          ALU.mult).then_inc(prodded, 1)
                        if not last:
                            dve.wait_ge(coefd, i * (NJ - 1) + j + 1)
                            dve.wait_ge(prodded, i * NJ + j + 1 + 2)
                            dve.tensor_tensor(hid[:, u, j, :], prod[:, j % 2, :], ps[:, 4 + j % 2, :], ALU.mult).then_inc(scaled, 1)
                        if j == 0 and m is not None:
                            normalise(m, slot % 2)
                    if m is not None:
                        keep_logits(m, slot)

                def residual(i):
                    dve.wait_ge(down, i + 1 + 2)
                    x_blk = k.X[:, bass.ds(i * TB, TB), :].rearrange("p t f -> p (t f)")
                    dve.scalar_tensor_tensor(out=x_blk, in0=ps[:, DOWN, :], scalar=0.5, in1=x_blk,
                                             op0=ALU.mult, op1=ALU.add).then_inc(resid, 1)
                    dve.wait_ge(resid, i + 1 + 1)
                    for c in range(TB):
                        tile_stats(k, dve, i * TB + c).then_inc(stats_done, 1)

                def step(s, g, r, ahead, route, spread, more):
                    if more:
                        products(s + 1, (r + 1) % 2, s + 1 + LEAD if ahead else None, (r + 1 + LEAD) % G)
                    if route:
                        routing(g + 1)
                    residual(s)

                chain(dve.memset(parts[:, :, 24:32], 0.0))
                normalise(0, 0)
                for m in range(LEAD):
                    if m + 1 < LEAD:
                        normalise(m + 1, (m + 1) % 2)
                    if m < G:
                        keep_logits(m, m)
                routing(0)
                keep_logits(LEAD - 1, (LEAD - 1) % G)
                products(0, 0, LEAD, LEAD % G)
                steps(dve, step)

            @block.scalar
            def _(act):
                ln_scale_act(k, act, var_ready, std_ready)

                def keep_x(m):
                    act.wait_ge(turned, m + 3)
                    if not (isinstance(m, int) and m == 0):
                        act.wait_ge(lg_done, m)
                    act.activation(xtp[:], ps[:, SHARED, :], ACT.Copy)
                    act.activation(xt[:, bass.ds(m * BLOCK, BLOCK)], ps[:, SHARED, :], ACT.Copy).then_inc(xt_kept, 1)

                def exponentials(g):
                    act.wait_ge(ex_in, g + 1)
                    act.activation(ex[:], ex[:], ACT.Exp).then_inc(ex_done, 1)

                def keep_coef(g):
                    act.wait_ge(coef_ps, g + 2)
                    act.activation(coef_t[:, bass.ds(g * (G * P), G * P)], ps[:, SHARED, :].bitcast(BF16)[:, 0:G * P], ACT.Copy).then_inc(coef_sb, 1)

                def silus(i, u, m):
                    for j in range(NJ):
                        act.wait_ge(gated, i * NJ + j + 1)
                        act.activation(silu[:, (u + j) % 2, :], ps[:, (u + j) % 2, :], ACT.Silu).then_inc(siluq, 1)
                        if j == 2 and m is not None:
                            keep_x(m)

                def step(s, g, r, ahead, route, spread, more):
                    if more:
                        silus(s + 1, (r + 1) % 2, s + 1 + LEAD if ahead else None)
                    if route:
                        exponentials(g + 1)
                    if spread:
                        keep_coef(g + 1)

                for m in range(LEAD):
                    keep_x(m)
                    if m == G - 1:
                        exponentials(0)
                keep_coef(0)
                silus(0, 0, LEAD)
                steps(act, step)

            @block.tensor
            def _(pe):
                def turn(m, v):
                    pe.wait_ge(xn_ready, m + 2)
                    pe.wait_ge(lg_kept, m + 1)
                    for c in range(TB):
                        last = pe.transpose(ps[:, SHARED, c * P:(c + 1) * P], xn[:, v, c, :], k.ident[:])
                    last.then_inc(turned, 1)

                def route_logits(m):
                    pe.wait_ge(xt_kept, m + 1)
                    for c in range(TB):
                        last = pe.matmul(ps[:, SHARED, c * E:(c + 1) * E], xtp[:, c * P:(c + 1) * P], router[:], start=True, stop=True)
                    last.then_inc(lg_done, 1)

                def turn_coef(g, kept):
                    pe.wait_ge(parts_ready, g + 1)
                    pe.wait_ge(lg_kept, kept + 1)
                    for b in range(G):
                        last = pe.transpose(ps[:, SHARED, :].bitcast(BF16)[:, b * P:(b + 1) * P],
                                            parts[:, b * TB:(b + 1) * TB, :].rearrange("p t c -> p (t c)"), k.ident_bf[:])
                    last.then_inc(coef_ps, 1)

                def ups(i, u, m, g):
                    x_in = xt[:, bass.ds(i * BLOCK, BLOCK)]
                    for j in range(NJ):
                        b = (u + j) % 2
                        pe.wait_ge(prodded, i * NJ + j + 1)
                        pe.matmul(ps[:, b, :], wg[:, j * P:(j + 1) * P], x_in, start=True, stop=True)
                        pe.matmul(ps[:, 2 + b, :], wu[:, j * P:(j + 1) * P], x_in, start=True, stop=True).then_inc(gated, 1)
                        if j < NJ - 1:
                            pe.wait_ge(scaled, i * (NJ - 1) + j + 1)
                            if j == 0:
                                pe.wait_ge(coef_sb, g + 1)
                            for c in range(TB):
                                last = pe.matmul(ps[:, 4 + j % 2, c * P:(c + 1) * P], sel[:, c * (NJ - 1) + j, :],
                                                 coef_t[:, bass.ds(i * P, P)], start=True, stop=True)
                            last.then_inc(coefd, 1)
                        if m is not None and j == 2:
                            turn(m, (u + LEAD) % 2)
                    if m is not None:
                        route_logits(m)

                def downs(i, u):
                    pe.wait_ge(scaled, i * (NJ - 1) + NJ - 1 + 2)
                    pe.wait_ge(prodded, i * NJ + NJ + 2)
                    pe.wait_ge(resid, i + 1)
                    for c in range(TB):
                        for j in range(NJ):
                            last = pe.matmul(ps[:, DOWN, c * D:(c + 1) * D], hid[:, u, j, c * P:(c + 1) * P], wd[:, j, :],
                                             start=(j == 0), stop=(j == NJ - 1))
                    last.then_inc(down, 1)

                def step(s, g, r, ahead, route, spread, more):
                    if more:
                        ups(s + 1, (r + 1) % 2, s + 1 + LEAD if ahead else None, g + (r + 1) // G)
                    if spread:
                        turn_coef(g + 1, s + 2 + LEAD if ahead else NBLK)
                    downs(s, r % 2)

                for credit, n in ((turned, 2), (down, 2), (coef_ps, 1)):
                    pe.sem_inc(credit, n)
                pe.wait_ge(w_rt, 32)
                for m in range(LEAD):
                    turn(m, m % 2)
                    route_logits(m)
                pe.wait_ge(w_in, 5 * 16)
                turn_coef(0, LEAD)
                ups(0, 0, LEAD, 0)
                pe.wait_ge(w_dn, 32)
                steps(pe, step)


def stage_scan(k, name, w, V, Y):
    nc = k.nc
    N = 16
    SEQ = 1024
    NB = k.tokens // SEQ
    with ExitStack() as ctx:
        sb = lambda n, shape, dt=F32: k.sb(f"{name}_{n}", shape, dt, ctx)
        xpw, dtw, vw = sb("xpw", [P, P]), sb("dtw", [P, D]), sb("vw", [P, D])
        vb = sb("vb", [P, D])
        normw, dtb, dp, a_neg = sb("normw", [P, 1]), sb("dtb", [P, 1]), sb("dp", [P, 1]), sb("a_neg", [P, N])
        sel = sb("sel", [96, 2 * N, P], BF16)
        scale2, shift2, rms = sb("scale2", [P, k.tiles]), sb("shift2", [P, k.tiles]), sb("rms", [P, 3, k.tiles])
        n_t = sb("n_t", [P, TB, D])
        xn = sb("xn", [P, 2, SEQ])
        bc, rest = sb("bc", [P, 2, SEQ], BF16), sb("rest", [P, BLOCK])
        dtx = rest
        z, ln, dd = (sb(n, [P, BLOCK]) for n in ("z", "ln", "dd"))
        dt, dtu = sb("dt", [P, 2, SEQ]), sb("dtu", [P, 2, SEQ])
        RS, RI, LAG = 4, 8, 3
        dec, inc = sb("dec", [P, RS, SEQ]), sb("inc", [P, RI, SEQ])
        c_copy = sb("c_copy", [P, SEQ])
        POOLED = [n for n in range(N) if n % 2 == 1]
        ps = k.ps
        two = lambda b: ps[:, b:b + 2, :].rearrange("p a b -> p (a b)")
        (w_in, var_ready, std_ready, dve_step, rms_in, rms_out, n_ready, t_n, n_copied,
         xp_done, dtx_ready, hi_ready, rest1, mid_ready, rest2, bc_ready, dt_ps, abs_done, z_ready, ln_ready, dt_max, d_done,
         dt_part, corr_done, dt_ready, dtu_ready, v_ps, v_read, dec_ready, b_done, c_done, inc_done, scanned, out_dve, out_pool, c_copied, summed,
         y_read, a_ready, setup) = k.sems(
            ctx, name, "w_in var_ready std_ready dve_step rms_in rms_out n_ready t_n n_copied "
            "xp_done dtx_ready hi_ready rest1 mid_ready rest2 bc_ready dt_ps abs_done z_ready ln_ready dt_max d_done "
            "dt_part corr_done dt_ready dtu_ready v_ps v_read dec_ready b_done c_done inc_done scanned out_dve out_pool c_copied summed "
            "y_read a_ready setup")
        PLAN = [("normalise", 2), ("turn", 2), ("copy", 3), ("xproj", 3), ("high", 4), ("rest", 4), ("mid", 5), ("last", 5), ("low", 6),
                ("dtproj", 4), ("positive", 5), ("exp", 5), ("ln", 5), ("one_off", 6), ("part", 6), ("softplus", 6), ("vproj", 5), ("vadd", 6)]
        SHIFT = 6

        def wait_out(engine, b, n):
            mine, done = ([c for c in range(N) if (c in POOLED) == (n % N in POOLED)], out_pool if n % N in POOLED else out_dve)
            engine.wait_ge(done, b * len(mine) + (mine.index(n % N) + 2 - (len(mine) if n < 0 else 0)))

        def sequences(engine, sequence):
            sequence(0, 0, True, True)
            with engine.Fori(0, NB // 2 - 1) as half:
                sequence(half * 2 + 1, 1, False, True)
                sequence(half * 2 + 2, 0, False, True)
            sequence(NB - 1, 1, False, False)

        def pieces(own, b, u, n):
            for q in range(2):
                for piece, at in PLAN:
                    if piece in own and at + q * SHIFT == n:
                        own[piece](b * 2 + q, b, u, q)

        def all_pieces(own):
            for n in range(16):
                pieces(own, 0, 0, n)

        with nc.Block() as block:
            @block.sync
            def _(sp):
                for dst, src in ((xpw[:, 0:32], w["xproj_t"][:, 8:40]), (xpw[:, 32:64], w["xproj_t"][:, 8:40]),
                                 (xpw[:, 64:96], w["xproj_t"][:, 8:40]), (xpw[:, 96:104], w["xproj_t"][:, 0:8]),
                                 (dtw[96:104, :], w["dt_wt"]), (vw[:], w["v_wt"]),
                                 (vb[:], w["v_b"].rearrange("(a n) -> a n", a=1).broadcast_to([P, D])),
                                 (normw[:], w["norm_w"].rearrange("(n a) -> n a", a=1)),
                                 (dtb[:], w["dt_b"].rearrange("(n a) -> n a", a=1)),
                                 (dp[:], w["D_p"].rearrange("(n a) -> n a", a=1)),
                                 (a_neg[:], w["A_log"]), (sel[:].rearrange("p a b -> p (a b)"), w["sel_bc"])):
                    sp.dma_start(dst, src).then_inc(w_in, 16)
                sp.wait_ge(w_in, 12 * 16)

            @block.vector
            def _(dve):
                step = chained(dve, dve_step)
                ln_scale_dve(k, dve, step, std_ready, var_ready)
                a, b, c = (rms[:, n, :] for n in range(3))
                step(dve.tensor_tensor(a, k.rstd[:], k.rstd[:], ALU.mult))
                step(dve.tensor_tensor(b, a, k.ln_tmp[:, 1, :], ALU.mult))
                step(dve.tensor_scalar(a, a, -EPS, EPS, ALU.mult, ALU.add))
                dve.tensor_tensor(b, b, a, ALU.add).then_inc(rms_in, 1)
                dve.wait_ge(rms_out, 1)
                step(dve.reciprocal(a, c))
                step(dve.tensor_tensor(c, a, a, ALU.mult))
                step(dve.tensor_tensor(c, c, b, ALU.mult))
                step(dve.tensor_scalar(c, c, -0.5, 1.5, ALU.mult, ALU.add))
                step(dve.tensor_tensor(a, a, c, ALU.mult))
                step(dve.tensor_tensor(shift2[:], k.shift[:], a, ALU.mult))
                step(dve.tensor_tensor(scale2[:], k.rstd[:], a, ALU.mult))
                dve.wait_ge(a_ready, 1)
                step(dve.tensor_scalar(a_neg[:], a_neg[:], -1.0, None, ALU.mult))
                dve.sem_inc(setup, 1)
                dve.sem_inc(inc_done, 1)
                dve.sem_inc(out_dve, 1)
                dve.sem_inc(y_read, 2)
                dve.sem_inc(v_read, 1)

                def rest_of_high(m, b, u, q):
                    cols = slice(q * BLOCK, (q + 1) * BLOCK)
                    for s in (32, 64):
                        dve.wait_ge(hi_ready, m + 1)
                        dve.tensor_tensor(rest[s:s + 32, :], ps[s:s + 32, 6, :], bc[s:s + 32, u, cols], ALU.subtract).then_inc(rest1, 1)

                def rest_of_mid(m, b, u, q):
                    cols = slice(q * BLOCK, (q + 1) * BLOCK)
                    dve.wait_ge(mid_ready, m * 2 + 2)
                    dve.tensor_tensor(rest[64:96, :], rest[64:96, :], bc[64:96, u, cols], ALU.subtract).then_inc(rest2, 1)

                def positive(m, b, u, q):
                    cols = slice(q * BLOCK, (q + 1) * BLOCK)
                    dve.wait_ge(dt_ps, m + 2)
                    dve.tensor_scalar(dt[:, u, cols], ps[:, 7, :], dtb[:, 0:1], 0.0, ALU.add, ALU.max).then_inc(dt_max, 1)

                def one_off(m, b, u, q):
                    dve.wait_ge(z_ready, m + 1)
                    dve.wait_ge(dt_ready, m + 1)
                    dve.tensor_scalar(dd[:], z[:], 1.0, -1.0, ALU.add, ALU.add).then_inc(d_done, 1)

                def part(m, b, u, q):
                    cols = slice(q * BLOCK, (q + 1) * BLOCK)
                    dve.wait_ge(ln_ready, m + 1)
                    dve.wait_ge(dt_max, m + 1)
                    dve.tensor_tensor(dt[:, u, cols], dt[:, u, cols], ln[:], ALU.add).then_inc(dt_part, 1)

                def vadd(m, b, u, q):
                    dve.wait_ge(v_ps, m + 1)
                    dve.tensor_tensor(V[:, bass.ds(m * TB, TB), :], ps[:, 6, :].rearrange("p (t f) -> p t f", f=D),
                                      vb[:].rearrange("p (a f) -> p a f", a=1).broadcast_to([P, TB, D]), ALU.add).then_inc(v_read, 1)

                own = dict(rest=rest_of_high, last=rest_of_mid, positive=positive, one_off=one_off, part=part, vadd=vadd)
                dve.sem_inc(dt_part, 1)

                def increment(b, u, n):
                    g = b * N + n
                    if n == 0:
                        dve.wait_ge(dtu_ready, b * 2 + 2)
                    dve.wait_ge(b_done, g + 1)
                    dve.wait_ge(summed, g + 1)
                    dve.tensor_tensor(inc[:, n % RI, :], dtu[:, u, :], two(0), ALU.mult).then_inc(inc_done, 1)

                def finish(b, u):
                    dve.wait_ge(summed, b * N + N + RI)
                    dve.scalar_tensor_tensor(out=Y[:, bass.ds(b * SEQ, SEQ)], in0=xn[:, u, :], scalar=dp[:, 0:1], in1=two(4),
                                             op0=ALU.mult, op1=ALU.add).then_inc(y_read, 1)

                def sequence(b, u, first, ahead):
                    for n in range(N):
                        g = b * N + n
                        if n == LAG and not first:
                            finish(b - 1, 1 - u)
                        dve.wait_ge(dec_ready, g + 1)
                        dve.wait_ge(inc_done, g + 2)
                        dve.tensor_tensor_scan(out=dec[:, n % RS, :], data0=dec[:, n % RS, :], data1=inc[:, n % RI, :], initial=0.0,
                                               op0=ALU.mult, op1=ALU.add).then_inc(scanned, 1)
                        if n < N - 1:
                            increment(b, u, n + 1)
                        elif ahead:
                            increment(b + 1, 1 - u, 0)
                        if n not in POOLED:
                            dve.wait_ge(c_done, g + 1)
                            dve.wait_ge(scanned, g + 1)
                            dve.tensor_tensor(inc[:, n % RI, :], dec[:, n % RS, :], two(2), ALU.mult).then_inc(out_dve, 1)
                        if ahead:
                            pieces(own, b + 1, 1 - u, n)
                    if not ahead:
                        finish(b, u)

                all_pieces(own)
                increment(0, 0, 0)
                sequences(dve, sequence)

            @block.scalar
            def _(act):
                ln_scale_act(k, act, var_ready, std_ready)
                act.wait_ge(rms_in, 1)
                act.activation(rms[:, 2, :], rms[:, 1, :], ACT.Sqrt).then_inc(rms_out, 1)
                act.wait_ge(w_in, 12 * 16)
                act.activation(a_neg[:], a_neg[:], ACT.Exp).then_inc(a_ready, 1)
                act.wait_ge(setup, 1)
                act.preload_act_table_set("natural_log_exp_and_others")

                def normalise(m, b, u, q):
                    act.wait_ge(t_n, m + 1)
                    for c in range(TB):
                        t = m * TB + c
                        act.activation(n_t[:, c, :], k.X[:, bass.ds(t, 1), :].rearrange("p a f -> p (a f)"), ACT.Identity,
                                       bias=shift2[:, bass.ds(t, 1)], scale=scale2[:, bass.ds(t, 1)]).then_inc(n_ready, 1)

                def copy(m, b, u, q):
                    act.wait_ge(t_n, m + 2)
                    act.wait_ge(y_read, b + 1)
                    act.activation(xn[:, u, q * BLOCK:(q + 1) * BLOCK], ps[:, 7, :], ACT.Copy, scale=normw[:, 0:1]).then_inc(n_copied, 1)

                def high(m, b, u, q):
                    cols = slice(q * BLOCK, (q + 1) * BLOCK)
                    act.wait_ge(xp_done, m + 1)
                    act.wait_ge(dt_ps, m + 1)
                    act.activation(dtx[96:104, :], ps[96:104, 6, :], ACT.Copy).then_inc(dtx_ready, 1)
                    act.activation(bc[0:96, u, cols], ps[0:96, 6, :], ACT.Copy).then_inc(hi_ready, 1)

                def mid(m, b, u, q):
                    cols = slice(q * BLOCK, (q + 1) * BLOCK)
                    for s in (32, 64):
                        act.wait_ge(rest1, m * 2 + 2)
                        act.activation(bc[s:s + 32, u, cols], rest[s:s + 32, :], ACT.Copy).then_inc(mid_ready, 1)

                def low(m, b, u, q):
                    cols = slice(q * BLOCK, (q + 1) * BLOCK)
                    act.wait_ge(rest2, m + 1)
                    act.activation(bc[64:96, u, cols], rest[64:96, :], ACT.Copy).then_inc(bc_ready, 1)

                def exp(m, b, u, q):
                    act.wait_ge(dt_max, m + 1)
                    act.wait_ge(corr_done, m + 1)
                    act.activation(z[:], ps[:, 7, :], ACT.Abs, bias=dtb[:, 0:1]).then_inc(abs_done, 1)
                    act.wait_ge(abs_done, m + 2)
                    act.activation(z[:], z[:], ACT.Exp, scale=-1.0).then_inc(z_ready, 1)

                def log(m, b, u, q):
                    act.wait_ge(z_ready, m + 1)
                    act.wait_ge(dt_part, m + 1)
                    act.activation(ln[:], z[:], ACT.Ln, bias=1.0).then_inc(ln_ready, 1)

                own = dict(normalise=normalise, copy=copy, high=high, mid=mid, low=low, exp=exp, ln=log)
                act.sem_inc(abs_done, 1)

                def decays(b, u, n):
                    if n == 0:
                        act.wait_ge(dt_ready, b * 2 + 3)
                    wait_out(act, b, n - RS)
                    act.activation(dec[:, n % RS, :], dt[:, u, :], ACT.Exp, scale=a_neg[:, n:n + 1]).then_inc(dec_ready, 1)

                def sequence(b, u, first, ahead):
                    for n in range(N):
                        if n + 2 < N:
                            decays(b, u, n + 2)
                        elif ahead:
                            decays(b + 1, 1 - u, n + 2 - N)
                        if n in POOLED:
                            act.wait_ge(c_done, b * N + n + 1)
                            wait_out(act, b, POOLED[POOLED.index(n) - 1] - (N if n == POOLED[0] else 0))
                            act.activation(c_copy[:], two(2), ACT.Copy).then_inc(c_copied, 1)
                        if ahead:
                            pieces(own, b + 1, 1 - u, n)

                all_pieces(own)
                act.wait_ge(setup, 1)
                for n in range(2):
                    act.wait_ge(dt_ready, 3)
                    act.activation(dec[:, n, :], dt[:, 0, :], ACT.Exp, scale=a_neg[:, n:n + 1]).then_inc(dec_ready, 1)
                sequences(act, sequence)

            @block.gpsimd
            def _(pool):
                def softplus(m, b, u, q):
                    cols = slice(q * BLOCK, (q + 1) * BLOCK)
                    pool.wait_ge(d_done, m + 1)
                    pool.tensor_tensor(dd[:], z[:], dd[:], ALU.subtract).then_inc(corr_done, 1)
                    pool.wait_ge(corr_done, m + 2)
                    pool.wait_ge(dt_part, m + 2)
                    pool.tensor_tensor(dt[:, u, cols], dt[:, u, cols], dd[:], ALU.add).then_inc(dt_ready, 1)
                    pool.wait_ge(dt_ready, m + 2)
                    pool.wait_ge(n_copied, m + 1)
                    pool.tensor_tensor(dtu[:, u, cols], dt[:, u, cols], xn[:, u, cols], ALU.mult).then_inc(dtu_ready, 1)

                own = dict(softplus=softplus)
                for credit in (dt_ready, corr_done):
                    pool.sem_inc(credit, 1)

                def sequence(b, u, first, ahead):
                    for n in range(N):
                        g = b * N + n
                        if n in POOLED:
                            pool.wait_ge(c_copied, b * len(POOLED) + POOLED.index(n) + 1)
                            pool.wait_ge(scanned, g + 1)
                            pool.tensor_tensor(inc[:, n % RI, :], dec[:, n % RS, :], c_copy[:], ALU.mult).then_inc(out_pool, 1)
                        if ahead:
                            pieces(own, b + 1, 1 - u, n)

                pool.sem_inc(out_pool, 1)
                all_pieces(own)
                sequences(pool, sequence)

            @block.tensor
            def _(pe):
                pe.wait_ge(w_in, 12 * 16)
                pe.sem_inc(summed, RI)

                def turn(m, b, u, q):
                    pe.wait_ge(n_ready, m * TB + TB)
                    pe.wait_ge(abs_done, m + 1)
                    for c in range(TB):
                        last = pe.transpose(ps[:, 7, c * P:(c + 1) * P], n_t[:, c, :], k.ident[:])
                    last.then_inc(t_n, 1)

                def xproj(m, b, u, q):
                    pe.wait_ge(v_read, m + 1)
                    pe.wait_ge(n_copied, m + 1)
                    pe.matmul(ps[0:104, 6, :], xpw[:, 0:104], xn[:, u, q * BLOCK:(q + 1) * BLOCK], start=True, stop=True).then_inc(xp_done, 1)

                def dtproj(m, b, u, q):
                    pe.wait_ge(dtx_ready, m + 1)
                    pe.matmul(ps[:, 7, :], dtw[96:104, :], dtx[96:104, :], start=True, stop=True).then_inc(dt_ps, 1)

                def vproj(m, b, u, q):
                    pe.wait_ge(rest1, m * 2 + 2)
                    for c in range(TB):
                        s = q * BLOCK + c * P
                        last = pe.matmul(ps[:, 6, c * D:(c + 1) * D], xn[:, u, s:s + P], vw[:], start=True, stop=True)
                    last.then_inc(v_ps, 1)

                own = dict(turn=turn, xproj=xproj, dtproj=dtproj, vproj=vproj)
                for credit in (t_n, dt_ps):
                    pe.sem_inc(credit, 1)

                def spread_b(b, u, n):
                    if n == 0:
                        pe.wait_ge(bc_ready, b * 2 + 2)
                    pe.wait_ge(inc_done, b * N + n + 1)
                    for h in range(2):
                        last = pe.matmul(ps[:, h, :], sel[:, n, :], bc[0:96, u, h * BLOCK:(h + 1) * BLOCK], start=True, stop=True)
                    last.then_inc(b_done, 1)

                def spread_c(b, u, n):
                    if (n - 1) % N in POOLED:
                        pe.wait_ge(c_copied, b * len(POOLED) + len([c for c in POOLED if c < n]))
                    else:
                        wait_out(pe, b, n - 1)
                    for h in range(2):
                        last = pe.matmul(ps[:, 2 + h, :], sel[:, N + n, :], bc[0:96, u, h * BLOCK:(h + 1) * BLOCK], start=True, stop=True)
                    last.then_inc(c_done, 1)

                def accumulate(b, n):
                    wait_out(pe, b, n)
                    if n == 0:
                        pe.wait_ge(y_read, b + 2)
                    for h in range(2):
                        last = pe.matmul(ps[:, 4 + h, :], k.ident[:], inc[:, n % RI, h * BLOCK:(h + 1) * BLOCK],
                                         start=(n == 0), stop=(n == N - 1))
                    last.then_inc(summed, 1)

                def sequence(b, u, first, ahead):
                    for n in range(N):
                        if first and n == 0:
                            for h in range(2):
                                last = pe.matmul(ps[:, 2 + h, :], sel[:, N, :], bc[0:96, u, h * BLOCK:(h + 1) * BLOCK], start=True, stop=True)
                            last.then_inc(c_done, 1)
                        else:
                            spread_c(b, u, n)
                        if n < N - 1:
                            spread_b(b, u, n + 1)
                        elif ahead:
                            spread_b(b + 1, 1 - u, 0)
                        if n >= LAG:
                            accumulate(b, n - LAG)
                        elif not first:
                            accumulate(b - 1, N - LAG + n)
                        if ahead:
                            pieces(own, b + 1, 1 - u, n)
                    if not ahead:
                        for n in range(N - LAG, N):
                            accumulate(b, n)

                all_pieces(own)
                spread_b(0, 0, 0)
                sequences(pe, sequence)


def stage_gated_attention(k, name, w, V, Y):
    nc = k.nc
    SEQ, CH = 1024, 256
    NB = k.tokens // SEQ
    NQ = SEQ // BLOCK
    NC = SEQ // CH
    with ExitStack() as ctx:
        sb = lambda n, shape, dt=F32: k.sb(f"{name}_{n}", shape, dt, ctx)
        mw, hw = sb("mw", [P, 4 * D]), sb("hw", [P, D])
        mb = sb("mb", [P, 4])
        hb, ub = sb("hb", [P, 1]), sb("ub", [P, 1])
        gam, bet = sb("gam", [P, 2]), sb("bet", [P, 2])
        rot = sb("rot", [P, 2, CH])
        alpha, abias = sb("alpha", [P, 4]), sb("abias", [P, 2, CH])
        bias = sb("bias", [P, 2 * CH])
        causal = sb("causal", [P, 2 * CH])
        vs = sb("vs", [P, 2, 2 * TB, D])
        ut, r = sb("ut", [P, 2, NQ, BLOCK]), sb("r", [P, 2, NQ, BLOCK])
        zt, q, kk = sb("zt", [P, NQ, BLOCK]), sb("q", [P, NQ, BLOCK]), sb("kk", [P, NQ, BLOCK])
        sc, pt = sb("sc", [P, NC, 3 * P]), sb("pt", [P, 2, 3 * P])
        top, den = sb("top", [P, NC, 2]), sb("den", [P, NC, 2])
        hr, hh, res = sb("hr", [P, NQ, BLOCK]), sb("hh", [P, NQ, BLOCK]), sb("res", [P, NQ, TB, D])
        ps = k.ps
        (w_in, prep, prepped, bias_ps, mx_ready, v_ready, z_ps, r_ps, u_ps, z_ready, r_ready, ut_ready, qk_ready, s_ps,
         s_read, top_ready, e_ready, den_ready, p_ready, pt_ps, pt_ready, h_ps, hr_ready, o_ps, hh_ready, res_ready, uh_ready, g_ps,
         kept, resid, stats_done, gate) = k.sems(
            ctx, name, "w_in prep prepped bias_ps mx_ready v_ready z_ps r_ps u_ps z_ready r_ready ut_ready qk_ready s_ps "
            "s_read top_ready e_ready den_ready p_ready pt_ps pt_ready h_ps hr_ready o_ps hh_ready res_ready uh_ready g_ps "
            "kept resid stats_done gate")

        def sequences(engine, sequence):
            sequence(0, 0, True, True)
            with engine.Fori(0, NB // 2 - 1) as half:
                sequence(half * 2 + 1, 1, False, True)
                sequence(half * 2 + 2, 0, False, True)
            sequence(NB - 1, 1, False, False)

        with nc.Block() as block:
            col = lambda a: a.rearrange("(n a) -> n a", a=1)
            loads = ((mw[:], w["mx_wt"]), (hw[:], w["h_wt"]), (hb[:], col(w["h_b"])), (rot[:].rearrange("p a b -> p (a b)"), w["rot"]),
                     (alpha[:], w["alpha"]), (causal[:], w["causal"]), (gam[:], w["gamma_t"]), (bet[:], w["beta_t"]),
                     (mb[:], w["mx_bt"]))

            @block.sync
            def _(sp):
                for dst, src in loads:
                    sp.dma_start(dst, src).then_inc(w_in, 16)
                sp.wait_ge(w_in, len(loads) * 16)

            @block.vector
            def _(dve):
                step = chained(dve, prep)
                dve.wait_ge(w_in, len(loads) * 16)
                for s in range(2):
                    step(dve.tensor_scalar(abias[:, s, :], rot[:, 1, :], alpha[:, 2 * s + 1:2 * s + 2], None, ALU.mult))
                    step(dve.scalar_tensor_tensor(out=abias[:, s, :], in0=rot[:, 0, :], scalar=alpha[:, 2 * s:2 * s + 1],
                                                  in1=abias[:, s, :], op0=ALU.mult, op1=ALU.add))
                step(dve.tensor_scalar(gam[:, 0:1], gam[:, 0:1], float(D) ** -0.5, None, ALU.mult))
                step(dve.tensor_scalar(bet[:, 0:1], bet[:, 0:1], float(D) ** -0.5, None, ALU.mult))
                step(dve.tensor_tensor(hb[:], hb[:], mb[:, 3:4], ALU.add))
                step(dve.tensor_scalar(ub[:], mb[:, 0:1], 0.5, None, ALU.mult))
                dve.sem_inc(prepped, 1)
                dve.wait_ge(bias_ps, 1)
                step(dve.tensor_tensor(bias[:], ps[:, 0, :], causal[:], ALU.add))
                dve.sem_inc(prepped, 1)
                for credit, n in ((s_read, 2), (pt_ready, 1), (hr_ready, 1), (resid, NQ), (uh_ready, 2), (kept, 2)):
                    dve.sem_inc(credit, n)

                def maxed(b, c):
                    g = b * NC + c
                    dve.wait_ge(s_ps, g + 2)
                    dve.wait_ge(pt_ps, g + 1)
                    dve.sem_inc(gate, 1)
                    for t, (a, z) in enumerate(((0, P), (P, 3 * P))):
                        last = dve.tensor_tensor_reduce(out=sc[:, c, a:z], in0=ps[:, 2 + c % 2, a:z], in1=bias[:, t * CH:t * CH + z - a],
                                                        scale=1.0, scalar=-BIG, op0=ALU.add, op1=ALU.max,
                                                        accum_out=top[:, c, t:t + 1])
                    last.then_inc(s_read, 1)
                    dve.wait_ge(s_read, g + 3)
                    dve.tensor_scalar(top[:, c, :], top[:, c, :], -1.0, None, ALU.mult).then_inc(top_ready, 1)

                def probabilities(b, c):
                    g = b * NC + c
                    dve.wait_ge(e_ready, g + 1)
                    dve.reciprocal(den[:, c, :], den[:, c, :]).then_inc(den_ready, 1)
                    dve.wait_ge(den_ready, g + 1)
                    dve.tensor_scalar(sc[:, c, 0:P], sc[:, c, 0:P], den[:, c, 0:1], None, ALU.mult)
                    dve.tensor_scalar(sc[:, c, P:3 * P], sc[:, c, P:3 * P], den[:, c, 1:2], None, ALU.mult).then_inc(p_ready, 1)

                def keep_turned(b, c):
                    g = b * NC + c
                    dve.wait_ge(pt_ps, g + 1 + NC)
                    dve.wait_ge(h_ps, g + 1)
                    dve.tensor_copy(pt[:, c % 2, :], ps[:, 4, 0:3 * P]).then_inc(pt_ready, 1)

                def gate_r(b, u, c):
                    g = b * NC + c
                    m, s = c // 2, (c % 2) * CH
                    dve.wait_ge(h_ps, g + 3)
                    dve.wait_ge(r_ready, b * NQ + m + 1)
                    dve.wait_ge(o_ps, b * NQ + 2)
                    dve.tensor_tensor(hr[:, m, s:s + CH], ps[:, 5, 0:CH], r[:, u, m, s:s + CH], ALU.mult).then_inc(hr_ready, 1)

                def gate_u(b, u, m):
                    g = b * NQ + m
                    dve.wait_ge(hh_ready, g + 1)
                    dve.wait_ge(ut_ready, g + 1)
                    dve.scalar_tensor_tensor(out=hh[:, m, :], in0=ut[:, u, m, :], scalar=1.0, in1=hh[:, m, :],
                                             op0=ALU.add, op1=ALU.mult).then_inc(uh_ready, 1)

                def residual(b, m):
                    g = b * NQ + m
                    flat = lambda a: a.rearrange("p t f -> p (t f)")
                    rs, x_blk = flat(res[:, m, :, :]), flat(k.X[:, bass.ds(g * TB, TB), :])
                    dve.wait_ge(g_ps, g + 1 + NQ)
                    dve.wait_ge(res_ready, g * TB + TB)
                    dve.scalar_tensor_tensor(out=rs, in0=ps[:, 7, :], scalar=1.0, in1=rs, op0=ALU.subtract, op1=ALU.mult).then_inc(kept, 1)
                    dve.scalar_tensor_tensor(out=x_blk, in0=ps[:, 6, :], scalar=0.5, in1=x_blk, op0=ALU.mult, op1=ALU.add).then_inc(kept, 1)
                    dve.wait_ge(kept, g * 2 + 4)
                    dve.scalar_tensor_tensor(out=x_blk, in0=rs, scalar=-0.5, in1=x_blk, op0=ALU.mult, op1=ALU.add).then_inc(resid, 1)
                    dve.wait_ge(resid, g + 1 + NQ)
                    for c in range(TB):
                        tile_stats(k, dve, g * TB + c).then_inc(stats_done, 1)

                def sequence(b, u, first, ahead):
                    maxed(b, 0)
                    maxed(b, 1)
                    probabilities(b, 0)
                    maxed(b, 2)
                    probabilities(b, 1)
                    maxed(b, 3)
                    probabilities(b, 2)
                    keep_turned(b, 0)
                    probabilities(b, 3)
                    keep_turned(b, 1)
                    if not first:
                        gate_u(b - 1, 1 - u, 0)
                        gate_u(b - 1, 1 - u, 1)
                    gate_r(b, u, 0)
                    keep_turned(b, 2)
                    gate_r(b, u, 1)
                    if not first:
                        residual(b - 1, 0)
                    keep_turned(b, 3)
                    gate_r(b, u, 2)
                    if not first:
                        residual(b - 1, 1)
                    gate_r(b, u, 3)

                sequences(dve, sequence)
                gate_u(NB - 1, 1, 0)
                gate_u(NB - 1, 1, 1)
                residual(NB - 1, 0)
                residual(NB - 1, 1)

            @block.scalar
            def _(act):
                def silu_m(b):
                    y_in = Y[:, bass.ds(b * SEQ, SEQ)]
                    act.activation(y_in, y_in, ACT.Silu).then_inc(mx_ready, 1)

                def silu_v(b, u):
                    if not (isinstance(b, int) and b < 2):
                        act.wait_ge(h_ps, b * NC + 2 - NC)
                    act.activation(vs[:, u, :, :], V[:, bass.ds(b * 2 * TB, 2 * TB), :], ACT.Silu).then_inc(v_ready, 1)

                def z_piece(b, m):
                    g = b * NQ + m
                    act.wait_ge(z_ps, g + 1)
                    act.wait_ge(qk_ready, g + 1)
                    act.activation(zt[:, m, :], ps[:, m, :], ACT.Silu, bias=mb[:, 1:2]).then_inc(z_ready, 1)

                def r_piece(b, u, m):
                    g = b * NQ + m
                    act.wait_ge(r_ps, g + 1)
                    act.wait_ge(hr_ready, b * NC + 1 - (NC if not isinstance(b, int) else min(NC, b * NC)))
                    act.activation(r[:, u, m, :], ps[:, m, :], ACT.Silu, bias=mb[:, 2:3]).then_inc(r_ready, 1)

                def u_piece(b, u, m):
                    g = b * NQ + m
                    act.wait_ge(u_ps, g + 1)
                    act.wait_ge(g_ps, g + 1)
                    act.activation(ut[:, u, m, :], ps[:, m, :], ACT.Tanh, bias=ub[:, 0:1], scale=0.5).then_inc(ut_ready, 1)

                def h_piece(b, m):
                    g = b * NQ + m
                    act.wait_ge(o_ps, g + 3)
                    act.wait_ge(g_ps, g + 1)
                    act.activation(hh[:, m, :], ps[:, 6 + m, :], ACT.Silu, bias=hb[:, 0:1]).then_inc(hh_ready, 1)

                def res_piece(b, m):
                    g = b * NQ + m
                    act.wait_ge(resid, g + 1)
                    for c in range(TB):
                        t = g * TB + c
                        act.activation(res[:, m, c, :], k.X[:, bass.ds(t, 1), :].rearrange("p a f -> p (a f)"), ACT.Identity,
                                       bias=k.shift[:, bass.ds(t, 1)], scale=k.rstd[:, bass.ds(t, 1)]).then_inc(res_ready, 1)

                def sequence(b, u, first, ahead):
                    if ahead:
                        silu_m(b + 1)
                    for c in range(NC):
                        g = b * NC + c
                        act.wait_ge(top_ready, g + 1)
                        act.activation(sc[:, c, 0:P], sc[:, c, 0:P], ACT.Exp, bias=top[:, c, 0:1], accum_out=den[:, c, 0:1])
                        act.activation(sc[:, c, P:3 * P], sc[:, c, P:3 * P], ACT.Exp, bias=top[:, c, 1:2],
                                       accum_out=den[:, c, 1:2]).then_inc(e_ready, 1)
                    if not first:
                        h_piece(b - 1, 0)
                        h_piece(b - 1, 1)
                    if ahead:
                        z_piece(b + 1, 0)
                        z_piece(b + 1, 1)
                    if not first:
                        res_piece(b - 1, 0)
                    if ahead:
                        r_piece(b + 1, 1 - u, 0)
                        r_piece(b + 1, 1 - u, 1)
                    if not first:
                        res_piece(b - 1, 1)
                    if ahead:
                        silu_v(b + 1, 1 - u)
                    u_piece(b, u, 0)
                    u_piece(b, u, 1)

                act.wait_ge(prepped, 2)
                silu_m(0)
                silu_v(0, 0)
                for m in range(NQ):
                    z_piece(0, m)
                for m in range(NQ):
                    r_piece(0, 0, m)
                sequences(act, sequence)
                for m in range(NQ):
                    h_piece(NB - 1, m)
                for m in range(NQ):
                    res_piece(NB - 1, m)

            @block.gpsimd
            def _(pool):
                pool.sem_inc(qk_ready, NQ)
                pool.wait_ge(prepped, 1)
                with pool.Fori(0, NB) as b:
                    for m in range(NQ):
                        g = b * NQ + m
                        pool.wait_ge(z_ready, g + 1)
                        pool.wait_ge(s_ps, b * NC + 1)
                        pool.sem_inc(gate, 1)
                        pool.tensor_scalar(q[:, m, :], zt[:, m, :], gam[:, 0:1], bet[:, 0:1], ALU.mult, ALU.add)
                        pool.tensor_scalar(kk[:, m, :], zt[:, m, :], gam[:, 1:2], bet[:, 1:2], ALU.mult, ALU.add).then_inc(qk_ready, 1)

            @block.tensor
            def _(pe):
                def product(part, b, m):
                    return pe.matmul(ps[:, m, :], mw[:, part * D:(part + 1) * D], Y[:, bass.ds((b * NQ + m) * BLOCK, BLOCK)], start=True, stop=True)

                def z_product(b, m):
                    pe.wait_ge(mx_ready, b + 1)
                    if not (isinstance(b, int) and b < 1):
                        pe.wait_ge(r_ready, b * NQ)
                    if not (isinstance(b, int) and b < 2):
                        pe.wait_ge(ut_ready, b * NQ + m + 1 - 2 * NQ)
                    product(1, b, m).then_inc(z_ps, 1)

                def r_product(b, m):
                    pe.wait_ge(z_ready, b * NQ + m + 1)
                    product(2, b, m).then_inc(r_ps, 1)

                def u_product(b, m, ahead):
                    if ahead:
                        pe.wait_ge(r_ready, b * NQ + m + 1 + NQ)
                    else:
                        pe.wait_ge(ut_ready, b * NQ + m + 1 - NQ)
                    product(0, b, m).then_inc(u_ps, 1)

                def scores(b, c):
                    g = b * NC + c
                    m, s = c // 2, (c % 2) * CH
                    pe.wait_ge(qk_ready, b * NQ + m + 1 + NQ)
                    pe.wait_ge(s_read, g + 1)
                    pe.matmul(ps[:, 2 + c % 2, 0:P], q[:, m, s:s + P], kk[:, m, s:s + P], start=True, stop=True)
                    pe.matmul(ps[:, 2 + c % 2, P:3 * P], q[:, m, s + P:s + 2 * P], kk[:, m, s:s + CH], start=True, stop=True).then_inc(s_ps, 1)

                def turn(b, c):
                    g = b * NC + c
                    pe.wait_ge(p_ready, g + 1)
                    pe.wait_ge(pt_ready, g + 1)
                    for t in range(3):
                        last = pe.transpose(ps[:, 4, t * P:(t + 1) * P], sc[:, c, t * P:(t + 1) * P], k.ident[:])
                    last.then_inc(pt_ps, 1)

                def values(b, u, c):
                    g = b * NC + c
                    pe.wait_ge(pt_ready, g + 2)
                    pe.wait_ge(v_ready, b + 1)
                    pe.wait_ge(hr_ready, g + 1)
                    pe.matmul(ps[:, 5, 0:CH], vs[:, u, 2 * c, :], pt[:, c % 2, 0:CH], start=True, stop=False)
                    pe.matmul(ps[:, 5, P:CH], vs[:, u, 2 * c + 1, :], pt[:, c % 2, CH:3 * P], start=False, stop=True).then_inc(h_ps, 1)

                def out_product(b, m):
                    pe.wait_ge(resid, b * NQ + NQ)
                    pe.matmul(ps[:, 6 + m, :], mw[:, 3 * D:4 * D], Y[:, bass.ds((b * NQ + m) * BLOCK, BLOCK)], start=True, stop=False)
                    pe.wait_ge(hr_ready, b * NC + 2 * m + 3)
                    pe.matmul(ps[:, 6 + m, :], hw[:], hr[:, m, :], start=False, stop=True).then_inc(o_ps, 1)

                def turn_out(b, u, m):
                    g = b * NQ + m
                    pe.wait_ge(uh_ready, b * NQ + 4)
                    pe.wait_ge(resid, g + NQ)
                    for c in range(TB):
                        pe.transpose(ps[:, 6, c * P:(c + 1) * P], hh[:, m, c * P:(c + 1) * P], k.ident[:])
                    for c in range(TB):
                        last = pe.transpose(ps[:, 7, c * P:(c + 1) * P], ut[:, u, m, c * P:(c + 1) * P], k.ident[:])
                    last.then_inc(g_ps, 1)

                def sequence(b, u, first, ahead):
                    for c in range(NC):
                        scores(b, c)
                    if not first:
                        out_product(b - 1, 0)
                        out_product(b - 1, 1)
                    if ahead:
                        z_product(b + 1, 0)
                        z_product(b + 1, 1)
                    turn(b, 0)
                    if ahead:
                        r_product(b + 1, 0)
                    turn(b, 1)
                    values(b, u, 0)
                    if ahead:
                        r_product(b + 1, 1)
                    turn(b, 2)
                    values(b, u, 1)
                    if not first:
                        turn_out(b - 1, 1 - u, 0)
                    u_product(b, 0, ahead)
                    turn(b, 3)
                    values(b, u, 2)
                    if not first:
                        turn_out(b - 1, 1 - u, 1)
                    u_product(b, 1, ahead)
                    values(b, u, 3)

                pe.wait_ge(prepped, 1)
                for t in range(2):
                    last = pe.matmul(ps[:, 0, t * CH:(t + 1) * CH], abias[:, 0, t * P:(t + 1) * P], abias[:, 1, :], start=True, stop=True)
                last.then_inc(bias_ps, 1)
                pe.wait_ge(prepped, 2)
                for credit, n in ((s_ps, 1), (pt_ps, NC), (h_ps, 2), (o_ps, 2), (g_ps, NQ)):
                    pe.sem_inc(credit, n)
                for m in range(NQ):
                    z_product(0, m)
                for m in range(NQ):
                    r_product(0, m)
                sequences(pe, sequence)
                out_product(NB - 1, 0)
                out_product(NB - 1, 1)
                turn_out(NB - 1, 1, 0)
                turn_out(NB - 1, 1, 1)


def stage_expert_ffn(k, name, w, n_dram, y_dram):
    nc = k.nc
    E, F = 8, 512
    NF = F // P
    T, NBLK = k.tiles, k.blocks
    ROWS = T + E
    WORK = T + E - 1
    MAGIC = 12582912.0
    W1N, W2N = F + NF, NF * D + D
    R = 4
    n_rows = n_dram.rearrange("(t p) f -> p t f", p=P)
    y_rows = y_dram.rearrange("(t p) f -> p t f", p=P)
    with ExitStack() as ctx:
        sb = lambda n, shape, dt=F32: k.sb(f"{name}_{n}", shape, dt, ctx)
        w1, w2 = sb("w1", [P, E, W1N]), sb("w2", [P, E, W2N])
        gather_row, scatter_row = sb("gather_row", [P, ROWS + R]), sb("scatter_row", [P, ROWS])
        expert = sb("expert", [P, ROWS], I32)
        ps = k.ps
        w1_in, w2_in = k.sems(ctx, name, "w1_in w2_in")
        n_stored = k.sems(ctx, name, "n_stored0 n_stored1")
        with ExitStack() as part:
            psb = lambda n, shape, dt=F32: k.sb(f"{name}_{n}", shape, dt, part)
            router, rb = psb("router", [P, E]), psb("rb", [P, E])
            xn, xtp = psb("xn", [P, 2, TB, D]), psb("xtp", [P, 2, BLOCK])
            em8, lg, tmp, cum, oh = (psb(n, [P, T, E]) for n in ("em8", "lg", "tmp", "cum", "oh"))
            zeros = psb("zeros", [P, T * E])
            oh_bf, before, ones = psb("oh_bf", [P, T, E], BF16), psb("before", [P, P], BF16), psb("ones", [P, P], BF16)
            top, slot, hi, lo = (psb(n, [P, T]) for n in ("top", "slot", "hi", "lo"))
            counts = psb("counts", [P, 4, E])
            row_no, trash_row, lane, token1 = psb("row_no", [P, ROWS]), psb("trash_row", [P, ROWS]), psb("lane", [P, P]), psb("token1", [P, T])
            past = psb("past", [P, ROWS, E])
            OG = 4
            oh_lo, oh_hi = psb("oh_lo", [P, 2, OG, P]), psb("oh_hi", [P, 2, OG, ROWS])
            logits = ps[:, 2, :].rearrange("p (t e) -> p t e", e=E)
            (w_in, var_ready, std_ready, dve_step, xn_scaled, xn_ready, turned, xtp_ready, lg_done, oh_ready, ranks,
             onehots, inverted, inverse, gate) = k.sems(
                part, name, "w_in var_ready std_ready dve_step xn_scaled xn_ready turned xtp_ready lg_done oh_ready ranks "
                "onehots inverted inverse gate")
            row = lambda a, n: a.rearrange("(a n) -> a n", a=1).broadcast_to([P, n])
            loads = ((router[:], w["router_w"]), (rb[:], row(w["router_b"], E)), (em8[:].rearrange("p t e -> p (t e)"), w["em8"]),
                     (before[:], w["before"]), (row_no[:], w["row_no"]), (trash_row[:], w["trash_row"]), (lane[:], w["lane"]),
                     (token1[:], w["token1"]))
            with nc.Block() as block:
                @block.gpsimd
                def _(pool):
                    pool.dma_start(w1[:, :, 0:F], w["W1"].rearrange("e d f -> d e f")).then_inc(w1_in, 16)
                    pool.dma_start(w1[:, :, F:W1N], w["b1_t"]).then_inc(w1_in, 16)
                    for e in range(E):
                        pool.dma_start(w2[:, e, 0:NF * D].rearrange("p (c d) -> p c d", d=D), w["W2"][e].rearrange("(c p) d -> p c d", p=P)).then_inc(w2_in, 16)
                        pool.dma_start(w2[:, e, NF * D:], w["b2"][e:e + 1, :].broadcast_to([P, D])).then_inc(w2_in, 16)

                @block.sync
                def _(sp):
                    for dst, src in loads:
                        sp.dma_start(dst, src).then_inc(w_in, 16)
                    with sp.Fori(0, NBLK // 2) as half:
                        for u in range(2):
                            i = half * 2 + u
                            sp.wait_ge(xn_ready, i + 1)
                            sp.dma_start(n_rows[:, bass.ds(i * TB, TB), :], xn[:, u, :, :]).then_inc(n_stored[u], 16)
                    sp.wait_ge(w_in, len(loads) * 16)
                    for u in range(2):
                        sp.wait_ge(n_stored[u], NBLK // 2 * 16 + 16)

                @block.vector
                def _(dve):
                    step = chained(dve, dve_step)
                    bc = lambda a: a.rearrange("p (t a) -> p t a", a=1).broadcast_to([P, T, E])
                    over_t = lambda a: a.rearrange("p (a e) -> p a e", a=1).broadcast_to([P, T, E])
                    ln_scale_dve(k, dve, step, std_ready, var_ready)
                    step(dve.memset(ones[:], 1.0))
                    step(dve.memset(zeros[:], 0.0))
                    step(dve.memset(gather_row[:, ROWS:], 0.0))
                    for u in range(2):
                        dve.sem_inc(n_stored[u], 16)
                    with dve.Fori(0, NBLK // 2) as half:
                        for u in range(2):
                            i = half * 2 + u
                            dve.wait_ge(turned, i + 1)
                            dve.wait_ge(n_stored[u], half * 16 + 16)
                            normalise_block(k, dve, xn[:, u, :, :], i, xn_scaled, xn_ready, i)
                    dve.wait_ge(lg_done, T + 2 * TB)
                    dve.wait_ge(w_in, len(loads) * 16)
                    step(dve.tensor_tensor(lg[:], logits, over_t(rb[:]), ALU.add))
                    step(dve.tensor_reduce(top[:], lg[:], AX.X, ALU.max))
                    step(dve.tensor_tensor(tmp[:], lg[:], bc(top[:]), ALU.is_equal))
                    step(dve.tensor_tensor(tmp[:], tmp[:], em8[:], ALU.mult))
                    step(dve.tensor_reduce(top[:], tmp[:], AX.X, ALU.min))
                    step(dve.tensor_tensor(oh[:], em8[:], bc(top[:]), ALU.is_equal))
                    dve.tensor_copy(oh_bf[:], oh[:]).then_inc(oh_ready, 1)
                    dve.wait_ge(ranks, 2)
                    rank = ps[:, 3, :].rearrange("p (t e) -> p t e", e=E)
                    total = ps[:, 4, :].rearrange("p (t e) -> p t e", e=E)
                    cum_et = cum[:].rearrange("p t e -> p (t e)").rearrange("p (e t) -> p e t", t=T)
                    step(dve.tensor_copy(tmp[:].rearrange("p t e -> p (t e)").rearrange("p (e t) -> p e t", t=T), total.rearrange("p t e -> p e t")))
                    step(dve.tensor_tensor_scan(cum[:].rearrange("p t e -> p (t e)"), tmp[:].rearrange("p t e -> p (t e)"), zeros[:], 0.0, ALU.add, ALU.add))
                    step(dve.tensor_tensor(tmp[:], cum[:], tmp[:], ALU.subtract))
                    first, n_tiles, first_tile, adjust = (counts[:, n, :] for n in range(4))
                    step(dve.memset(counts[:], 0.0))
                    step(dve.tensor_copy(first[:, 1:E], cum_et[:, 0:E - 1, T - 1]))
                    step(dve.tensor_tensor(n_tiles, cum_et[:, :, T - 1], first, ALU.subtract))
                    step(dve.tensor_scalar(n_tiles, n_tiles, 1.0 / P, 0.5 - 0.5 / P, ALU.mult, ALU.add))
                    step(dve.tensor_scalar(n_tiles, n_tiles, MAGIC, None, ALU.add))
                    step(dve.tensor_scalar(n_tiles, n_tiles, -MAGIC, None, ALU.add))
                    for e in range(1, E):
                        step(dve.tensor_tensor(first_tile[:, e:e + 1], first_tile[:, e - 1:e], n_tiles[:, e - 1:e], ALU.add))
                    step(dve.scalar_tensor_tensor(out=adjust, in0=first_tile, scalar=float(P), in1=first, op0=ALU.mult, op1=ALU.subtract))
                    step(dve.tensor_tensor(lg[:], tmp[:].rearrange("p t e -> p (t e)").rearrange("p (e t) -> p t e", t=T), rank, ALU.add))
                    step(dve.tensor_tensor(lg[:], lg[:], over_t(adjust), ALU.add))
                    step(dve.tensor_tensor(lg[:], lg[:], oh[:], ALU.mult))
                    step(dve.tensor_reduce(slot[:], lg[:], AX.X, ALU.add))
                    step(dve.tensor_scalar(hi[:], slot[:], 1.0 / P, -0.5 + 0.5 / P, ALU.mult, ALU.add))
                    step(dve.tensor_scalar(hi[:], hi[:], MAGIC, None, ALU.add))
                    step(dve.tensor_scalar(hi[:], hi[:], -MAGIC, None, ALU.add))
                    step(dve.scalar_tensor_tensor(out=lo[:], in0=hi[:], scalar=-float(P), in1=slot[:], op0=ALU.mult, op1=ALU.add))
                    dve.sem_inc(inverted, 2)
                    per_tile = lambda a, t, n: a[:, bass.ds(t, OG)].rearrange("p (t a) -> p t a", a=1).broadcast_to([P, OG, n])
                    same = lambda a, n: a[:].rearrange("p (a n) -> p a n", a=1).broadcast_to([P, OG, n])
                    with dve.Fori(0, T // OG // 2) as half:
                        for u in range(2):
                            i = half * 2 + u
                            dve.wait_ge(inverted, i + 1)
                            dve.tensor_tensor(oh_hi[:, u, :, :], same(row_no, ROWS), per_tile(hi, i * OG, ROWS), ALU.is_equal).then_inc(onehots, 1)
                            dve.tensor_tensor(oh_lo[:, u, :, :], same(lane, P), per_tile(lo, i * OG, P), ALU.is_equal).then_inc(onehots, 1)
                            dve.wait_ge(onehots, i * 3 + 1)
                            dve.tensor_tensor(oh_hi[:, u, :, :], oh_hi[:, u, :, :], per_tile(token1, i * OG, ROWS), ALU.mult).then_inc(onehots, 1)
                    step(dve.tensor_tensor(past[:], row_no[:].rearrange("p (t a) -> p t a", a=1).broadcast_to([P, ROWS, E]),
                                           first_tile.rearrange("p (a e) -> p a e", a=1).broadcast_to([P, ROWS, E]), ALU.is_ge))
                    step(dve.tensor_reduce(gather_row[:, 0:ROWS], past[:], AX.X, ALU.add))
                    step(dve.tensor_scalar(expert[:], gather_row[:, 0:ROWS], -1.0, None, ALU.add))
                    dve.wait_ge(inverse, 1)
                    step(dve.tensor_copy(gather_row[:, 0:ROWS], ps[:, 5, 0:ROWS]))
                    step(dve.scalar_tensor_tensor(out=scatter_row[:], in0=gather_row[:, 0:ROWS], scalar=0.0, in1=trash_row[:], op0=ALU.is_equal, op1=ALU.mult))
                    step(dve.scalar_tensor_tensor(out=scatter_row[:], in0=scatter_row[:], scalar=-1.0, in1=gather_row[:, 0:ROWS], op0=ALU.add, op1=ALU.add))
                    step(dve.tensor_scalar(gather_row[:, 0:ROWS], gather_row[:, 0:ROWS], -1.0, 0.0, ALU.add, ALU.max))

                @block.scalar
                def _(act):
                    ln_scale_act(k, act, var_ready, std_ready)
                    act.sem_inc(xtp_ready, 2)
                    with act.Fori(0, NBLK // 2) as half:
                        for u in range(2):
                            i = half * 2 + u
                            act.wait_ge(turned, i + 3)
                            act.wait_ge(lg_done, i * TB + TB)
                            act.activation(xtp[:, u, :], ps[:, u, :], ACT.Copy).then_inc(xtp_ready, 1)

                @block.tensor
                def _(pe):
                    pe.sem_inc(turned, 2)
                    pe.sem_inc(lg_done, 2 * TB)
                    pe.wait_ge(w_in, len(loads) * 16)
                    def turn(i, u):
                        pe.wait_ge(xn_ready, i + 1)
                        pe.wait_ge(xtp_ready, i + 1)
                        for c in range(TB):
                            last = pe.transpose(ps[:, u, c * P:(c + 1) * P], xn[:, u, c, :], k.ident[:])
                        last.then_inc(turned, 1)

                    def route_logits(i, u):
                        pe.wait_ge(xtp_ready, i + 3)
                        for c in range(TB):
                            pe.matmul(ps[:, 2, bass.ds((i * TB + c) * E, E)], xtp[:, u, c * P:(c + 1) * P], router[:],
                                      start=True, stop=True).then_inc(lg_done, 1)

                    turn(0, 0)
                    with pe.Fori(0, NBLK // 2 - 1) as half:
                        for u in range(2):
                            turn(half * 2 + u + 1, 1 - u)
                            route_logits(half * 2 + u, u)
                    turn(NBLK - 1, 1)
                    route_logits(NBLK - 2, 0)
                    route_logits(NBLK - 1, 1)
                    pe.wait_ge(oh_ready, 1)
                    flat = oh_bf[:].rearrange("p t e -> p (t e)")
                    pe.matmul(ps[:, 3, :], before[:], flat, start=True, stop=True).then_inc(ranks, 1)
                    pe.matmul(ps[:, 4, :], ones[:], flat, start=True, stop=True).then_inc(ranks, 1)
                    pe.matmul(ps[:, 5, 0:ROWS], zeros[:, 0:P], zeros[:, 0:ROWS], start=True, stop=False)
                    with pe.Fori(0, T // OG // 2) as half:
                        for u in range(2):
                            pe.wait_ge(onehots, (half * 2 + u) * 3 + 3)
                            for t in range(OG):
                                last = pe.matmul(ps[:, 5, 0:ROWS], oh_lo[:, u, t, :], oh_hi[:, u, t, :], start=False, stop=False)
                            last.then_inc(inverted, 1)
                    pe.matmul(ps[:, 5, 0:ROWS], zeros[:, 0:P], zeros[:, 0:ROWS], start=False, stop=True).then_inc(inverse, 1)

        xg, xt = sb("xg", [P, R, D]), sb("xt", [P, 2, P])
        w1e, w2e = sb("w1e", [P, 2, W1N]), sb("w2e", [P, 2, W2N])
        hid, yt = sb("hid", [P, 2, F]), sb("yt", [P, R, D])
        g_idx, s_idx = sb("g_idx", [P, R], mybir.dt.uint32), sb("s_idx", [P, R], mybir.dt.uint32)
        (idx_ready, turned, xt_ready, w1_ready, w2_ready, up, gelu, down, y_ready, gate) = k.sems(
            ctx, name + "b", "idx_ready turned xt_ready w1_ready w2_ready up gelu down y_ready gate")
        gathered = k.sems(ctx, name + "b", " ".join(f"gathered{r}" for r in range(R)))
        scattered = k.sems(ctx, name + "b", " ".join(f"scattered{r}" for r in range(R)))
        PEEL = WORK % R + R

        def hidden(c, s):
            return ps[:, 2 + s + 4 * (c // 2), (c % 2) * P:(c % 2 + 1) * P]

        def tiles(engine, body, first=0):
            for m in range(first, PEEL):
                body(m, m % R, m // R)
            with engine.Fori(0, (WORK - PEEL) // R) as turn:
                for v in range(R):
                    body(turn * R + (PEEL + v), (PEEL + v) % R, turn + (PEEL + v) // R)

        with nc.Block() as block:
            @block.gpsimd
            def _(pool):
                def gather(m, r):
                    pool.wait_ge(idx_ready, m + 1)
                    pool.sem_inc(gate, 1)
                    pool.indirect_dma_start(xg[:, r, :], None, n_dram[:, :], bass.IndirectOffsetOnAxis(g_idx[:, r:r + 1], 0)).then_inc(gathered[r], 16)

                def scatter(m, r):
                    pool.wait_ge(y_ready, m + 1)
                    pool.sem_inc(gate, 1)
                    pool.indirect_dma_start(y_dram[:, :], bass.IndirectOffsetOnAxis(s_idx[:, r:r + 1], 0), yt[:, r, :], None).then_inc(scattered[r], 16)

                for m in range(R):
                    gather(m, m)
                with pool.Fori(0, (ROWS - R) // R) as turn:
                    for r in range(R):
                        gather(turn * R + (R + r), r)
                        scatter(turn * R + r, r)
                for m in range(ROWS - R, WORK):
                    scatter(m, m % R)
                for r in range(R):
                    pool.wait_ge(scattered[r], (WORK + R - 1 - r) // R * 16)

            @block.vector
            def _(dve):
                def finish(m, r, s, q):
                    dve.wait_ge(down, m + 3)
                    if not (isinstance(q, int) and q == 0):
                        dve.wait_ge(scattered[r], q * 16)
                    dve.tensor_copy(s_idx[:, r:r + 1], scatter_row[:, bass.ds(m, 1)])
                    dve.tensor_tensor(yt[:, r, :], ps[:, 4 + s, 0:D], w2e[:, s, NF * D:], ALU.add).then_inc(y_ready, 1)

                def body(m, r, q):
                    s = r % 2
                    e = dve.value_load(expert[0:1, bass.ds(m, 1)], min_val=0, max_val=E - 1)
                    dve.wait_ge(gelu, (m + 1) * NF)
                    dve.tensor_copy(w1e[:, s, :], w1[:, bass.ds(e, 1), :].rearrange("p a f -> p (a f)")).then_inc(w1_ready, 1)
                    if not (isinstance(m, int) and m < 2):
                        finish(m - 2, (r - 2) % R, s, q + (r - 2) // R)
                        dve.wait_ge(y_ready, m - 1)
                    dve.tensor_copy(w2e[:, s, :], w2[:, bass.ds(e, 1), :].rearrange("p a f -> p (a f)")).then_inc(w2_ready, 1)
                    dve.wait_ge(turned, m + 1)
                    dve.tensor_copy(g_idx[:, r:r + 1], gather_row[:, bass.ds(m + R, 1)]).then_inc(idx_ready, 1)

                dve.wait_ge(w1_in, 2 * 16)
                dve.wait_ge(w2_in, 2 * E * 16)
                dve.tensor_copy(g_idx[:], gather_row[:, 0:R]).then_inc(idx_ready, R)
                dve.sem_inc(gelu, 2 * NF)
                dve.sem_inc(down, 2)
                tiles(dve, body)
                for m in (WORK - 2, WORK - 1):
                    finish(m, m % R, m % 2, m // R)

            @block.scalar
            def _(act):
                def copy_x(m, s):
                    act.wait_ge(turned, m + 1)
                    act.wait_ge(up, m * NF)
                    act.activation(xt[:, s, :], ps[:, s, 0:P], ACT.Copy).then_inc(xt_ready, 1)

                def body(m, r, q):
                    s = r % 2
                    for c in range(NF):
                        act.wait_ge(up, m * NF + (c // 2 + 1) * 2 + 2 * NF)
                        act.wait_ge(down, m + 1)
                        act.activation(hid[:, s, c * P:(c + 1) * P], hidden(c, s), ACT.Gelu,
                                       bias=w1e[:, s, F + c:F + c + 1]).then_inc(gelu, 1)
                        if c == 0:
                            copy_x(m + 1, 1 - s)

                act.sem_inc(up, 2 * NF)
                copy_x(0, 0)
                tiles(act, body)

            @block.tensor
            def _(pe):
                def turn(m, r, s, q):
                    pe.wait_ge(gathered[r], q * 16 + 16)
                    pe.wait_ge(xt_ready, m - 1 if not isinstance(m, int) else max(m - 1, 0))
                    pe.sem_inc(gate, 1)
                    pe.transpose(ps[:, s, 0:P], xg[:, r, :], k.ident[:]).then_inc(turned, 1)

                def body(m, r, q):
                    s = r % 2
                    pe.wait_ge(w1_ready, m + 1)
                    pe.wait_ge(xt_ready, m + 1)
                    pe.wait_ge(gelu, (m + 1) * NF)
                    for c in range(NF):
                        pe.matmul(hidden(c, s), w1e[:, s, c * P:(c + 1) * P], xt[:, s, :], start=True, stop=True).then_inc(up, 1)
                    turn(m + 1, (r + 1) % R, 1 - s, q + (r + 1) // R)
                    if not (isinstance(m, int) and m < 1):
                        downs(m - 1, 1 - s)

                def downs(m, s):
                    pe.wait_ge(gelu, (m + 3) * NF)
                    pe.wait_ge(w2_ready, m + 1)
                    pe.wait_ge(y_ready, m - 1 if not isinstance(m, int) else max(m - 1, 0))
                    for c in range(NF):
                        last = pe.matmul(ps[:, 4 + s, 0:D], hid[:, s, c * P:(c + 1) * P], w2e[:, s, c * D:(c + 1) * D],
                                         start=c == 0, stop=c == NF - 1)
                    last.then_inc(down, 1)

                turn(0, 0, 0, 0)
                tiles(pe, body)
                downs(WORK - 1, (WORK - 1) % 2)

        y_in = sb("y_in", [P, R, TB, D])
        y_loaded = k.sems(ctx, name, " ".join(f"y_loaded{r}" for r in range(R)))
        resid, stats_done = k.sems(ctx, name + "c", "resid stats_done")
        with nc.Block() as block:
            @block.sync
            def _(sp):
                for i in range(NBLK):
                    if i >= R:
                        sp.wait_ge(resid, i - R + 1)
                    sp.dma_start(y_in[:, i % R, :, :], y_rows[:, i * TB:(i + 1) * TB, :]).then_inc(y_loaded[i % R], 16)

            @block.vector
            def _(dve):
                for i in range(NBLK):
                    x_blk = k.X[:, i * TB:(i + 1) * TB, :]
                    dve.wait_ge(y_loaded[i % R], (i // R + 1) * 16)
                    dve.scalar_tensor_tensor(out=x_blk, in0=y_in[:, i % R, :, :], scalar=0.5, in1=x_blk, op0=ALU.mult, op1=ALU.add).then_inc(resid, 1)
                    dve.wait_ge(resid, i + 1)
                    for t in range(i * TB, (i + 1) * TB):
                        dve.bn_stats(k.stats[:, t, :], k.X[:, t, :]).then_inc(stats_done, 1)


def stage_kernel_attention(k, name, w):
    nc = k.nc
    SEQ, SH, RF, NM = 1024, 64, 32, 5
    NF = 2 * RF
    NT = SEQ // P
    NB = k.tokens // SEQ
    T, NBLK = k.tiles, k.blocks
    TWO_PI = 2 * np.pi
    MAGIC = 12582912.0
    C1 = 6.28125
    C2 = float(np.float32(np.round((TWO_PI - C1) * 2 ** 21) / 2 ** 21))
    C3 = float(np.float32(TWO_PI - C1 - C2))
    PI_IN = 3.1415925
    mags = [float(np.sqrt(np.float32(abs((-1.0) ** m / f) + 1e-10))) for m, f in enumerate((1, 1, 2, 6, 24))]
    scale = float(np.sqrt(2.0 / (2 * RF)) * np.sqrt(np.exp(-0.5)))
    with ExitStack() as ctx:
        sb = lambda n, shape, dt=F32: k.sb(f"{name}_{n}", shape, dt, ctx)
        sem = lambda names: k.sems(ctx, name, names)
        AT_CH, AT_PR, AT_V, NCOL = SH, SH + 1, SH + 1 + RF, SH + 1 + RF + D
        all_w, all_b = sb("all_w", [P, NCOL]), sb("all_b", [P, NCOL])
        wc = sb("wc", [P, 3, SH])
        brf = sb("brf", [P, RF])
        decay, mask = sb("decay", [P, SEQ]), sb("mask", [P, P], BF16)
        temp = sb("temp", [P, 4])
        prod = sb("prod", [P, T, NCOL])
        shell, proj, vw = prod[:, :, 0:SH], prod[:, :, AT_PR:AT_V], prod[:, :, AT_V:NCOL]
        feats = sb("feats", [P, T, NF])
        powers = sb("powers", [P, T, NM])
        ps = k.ps
        row = lambda a, n: a.rearrange("(a n) -> a n", a=1).broadcast_to([P, n])
        with ExitStack() as part:
            psb = lambda n, shape, dt=F32: k.sb(f"{name}_{n}", shape, dt, part)
            xn, xt = psb("xn", [P, 2, TB, D]), psb("xt", [P, 2, BLOCK])
            ws, wv, wo, om = psb("ws", [SH, D]), psb("wv", [P, D]), psb("wo", [P, D]), psb("om", [SH, RF])
            bsh, bv, bo = psb("bsh", [SH, P]), psb("bv", [P, P]), psb("bo", [P, D])
            (w_in, var_ready, std_ready, dve_step, spread, folded, w_ready, xn_ready, turned, xt_ready, prod_ps, prod_ready) = sem(
                "w_in var_ready std_ready dve_step spread folded w_ready xn_ready turned xt_ready prod_ps prod_ready")
            col = lambda a: a.rearrange("(n a) -> n a", a=1)
            bcol = psb("bcol", [P, 2])
            with nc.Block() as block:
                loads = ((all_w[:, 0:SH], w["shell_t"]), (all_w[:, AT_CH:AT_CH + 1], w["charge_t"]), (ws[:], w["shell"]), (wv[:], w["v"]),
                         (wo[:], w["out_t"]), (om[:], w["omega_t"]),
                         (wc[:, 0:2, :], w["combine_t"][0:256, :].rearrange("(c p) n -> p c n", p=P)),
                         (wc[0:SH, 2, :], w["combine_t"][256:320, :]), (all_b[:, 0:SH], row(w["b_shell"], SH)),
                         (all_b[:, AT_CH:AT_CH + 1], row(w["b_charge"], 1)), (bcol[:, 0:1], col(w["b_v"])), (bcol[0:SH, 1:2], col(w["b_shell"])),
                         (bo[:], row(w["b_out"], D)), (brf[:], row(w["rff_bias"], RF)), (decay[:], w["decay"]),
                         (mask[:], w["mask"]), (temp[:, 0:1], row(w["log_temp"], 1)))

                @block.sync
                def _(sp):
                    for dst, src in loads:
                        sp.dma_start(dst, src).then_inc(w_in, 16)
                    sp.wait_ge(w_in, len(loads) * 16)

                @block.vector
                def _(dve):
                    step = chained(dve, dve_step)
                    ln_scale_dve(k, dve, step, std_ready, var_ready)
                    dve.wait_ge(w_in, len(loads) * 16)
                    step(dve.tensor_copy(bv[:], bcol[:, 0:1].broadcast_to([P, P])))
                    step(dve.tensor_copy(bsh[:], bcol[0:SH, 1:2].broadcast_to([SH, P])))
                    dve.sem_inc(spread, 1)
                    dve.wait_ge(folded, 1)
                    step(dve.tensor_copy(all_w[:, AT_PR:AT_V], ps[:, 7, 0:RF]))
                    step(dve.tensor_copy(all_w[:, AT_V:NCOL], ps[:, 7, RF:RF + D]))
                    step(dve.tensor_copy(all_b[:, AT_PR:AT_V], ps[:, 6, 0:RF]))
                    step(dve.tensor_tensor(all_b[:, AT_V:NCOL], ps[:, 6, RF:RF + D], bo[:], ALU.add))
                    dve.sem_inc(w_ready, 1)
                    dve.sem_inc(prod_ready, 4)
                    bias = all_b[:].rearrange("p (a f) -> p a f", a=1).broadcast_to([P, 2, NCOL])

                    def normalise(i, u):
                        dve.wait_ge(turned, i + 1)
                        for c in range(TB):
                            normalised(k, dve, xn[:, u, c, :], i * TB + c).then_inc(xn_ready, 1)

                    def keep(i, u):
                        for h in range(2):
                            dve.wait_ge(prod_ps, i * 2 + h + 1)
                            dve.tensor_tensor(prod[:, bass.ds(i * TB + 2 * h, 2), :], ps[:, 2 + 2 * u + h, 0:2 * NCOL].rearrange("p (t f) -> p t f", t=2),
                                              bias, ALU.add).then_inc(prod_ready, 1)

                    normalise(0, 0)
                    normalise(1, 1)
                    with dve.Fori(0, NBLK // 2 - 1) as half:
                        for u in range(2):
                            normalise(half * 2 + u + 2, u)
                            keep(half * 2 + u, u)
                    for u in range(2):
                        keep(NBLK - 2 + u, u)

                @block.scalar
                def _(act):
                    ln_scale_act(k, act, var_ready, std_ready)
                    act.sem_inc(xt_ready, 2)
                    with act.Fori(0, NBLK // 2) as half:
                        for u in range(2):
                            i = half * 2 + u
                            act.wait_ge(turned, i + 3)
                            act.wait_ge(prod_ready, i * 2 + 1)
                            act.activation(xt[:, u, :], ps[:, u, :], ACT.Copy).then_inc(xt_ready, 1)

                @block.tensor
                def _(pe):
                    def turn(i, u):
                        pe.wait_ge(xn_ready, i * TB + TB)
                        pe.wait_ge(xt_ready, i + 1)
                        for c in range(TB):
                            last = pe.transpose(ps[:, u, c * P:(c + 1) * P], xn[:, u, c, :], k.ident[:])
                        last.then_inc(turned, 1)

                    def products(i, u):
                        pe.wait_ge(xt_ready, i + 3)
                        for h in range(2):
                            pe.wait_ge(prod_ready, i * 2 + h + 1)
                            for c in range(2):
                                t = 2 * h + c
                                last = pe.matmul(ps[:, 2 + 2 * u + h, c * NCOL:(c + 1) * NCOL], xt[:, u, t * P:(t + 1) * P], all_w[:], start=True, stop=True)
                            last.then_inc(prod_ps, 1)

                    pe.wait_ge(w_in, len(loads) * 16)
                    pe.wait_ge(spread, 1)
                    pe.matmul(ps[:, 7, 0:RF], ws[:], om[:], start=True, stop=True)
                    pe.matmul(ps[:, 7, RF:RF + D], wv[:], wo[:], start=True, stop=True)
                    pe.matmul(ps[:, 6, 0:RF], bsh[:], om[:], start=True, stop=True)
                    pe.matmul(ps[:, 6, RF:RF + D], bv[:], wo[:], start=True, stop=True).then_inc(folded, 1)
                    pe.sem_inc(turned, 2)
                    turn(0, 0)
                    pe.wait_ge(w_ready, 1)
                    with pe.Fori(0, NBLK // 2 - 1) as half:
                        for u in range(2):
                            turn(half * 2 + u + 1, 1 - u)
                            products(half * 2 + u, u)
                    turn(NBLK - 1, 1)
                    products(NBLK - 2, 0)
                    products(NBLK - 1, 1)

        with ExitStack() as part:
            psb = lambda n, shape, dt=F32: k.sb(f"{name}_{n}", shape, dt, part)
            ang, turns, sq = psb("ang", [P, T, RF]), psb("turns", [P, T, RF]), psb("sq", [P, T, SH])
            norm = psb("norm", [P, T])
            charge = prod[:, :, AT_CH]
            dve_b, norm2, norm_ready, reduced, abs_done, sines, tanhed, expd, lnd = sem("dve_b norm2 norm_ready reduced abs_done sines tanhed expd lnd")
            bc = lambda a: a.rearrange("p (t a) -> p t a", a=1).broadcast_to([P, T, RF])
            half_pi = psb("half_pi", [P, 1])
            with nc.Block() as block:
                @block.vector
                def _(dve):
                    step = chained(dve, dve_b)
                    step(dve.tensor_tensor(sq[:], shell, shell, ALU.mult))
                    dve.tensor_reduce(norm[:], sq[:], AX.X, ALU.add).then_inc(norm2, 1)
                    step(dve.memset(half_pi[:], float(np.pi / 2)))
                    dve.wait_ge(lnd, 1)
                    z, one_z, ln_z, v = (temp[:, n:n + 1] for n in (1, 2, 3, 0))
                    step(dve.tensor_scalar(one_z, one_z, -1.0, None, ALU.add))
                    step(dve.tensor_tensor(one_z, z, one_z, ALU.subtract))
                    step(dve.tensor_tensor(ln_z, ln_z, one_z, ALU.add))
                    step(dve.tensor_scalar(v, v, 0.0, 0.1, ALU.max, ALU.add))
                    step(dve.tensor_tensor(v, v, ln_z, ALU.add))
                    step(dve.reciprocal(v, v))
                    step(dve.tensor_scalar(decay[:], decay[:], v, None, ALU.mult))
                    dve.wait_ge(norm_ready, 1)
                    root = sq[:, :, 0]
                    step(dve.tensor_scalar(root, root, 1e-12, None, ALU.max))
                    step(dve.reciprocal(sq[:, :, 1], root))
                    step(dve.tensor_scalar(norm[:], norm[:], 1e-24, None, ALU.max))
                    step(dve.tensor_tensor(root, sq[:, :, 1], sq[:, :, 1], ALU.mult))
                    step(dve.tensor_tensor(root, root, norm[:], ALU.mult))
                    step(dve.tensor_scalar(root, root, -0.5, 1.5, ALU.mult, ALU.add))
                    step(dve.tensor_tensor(norm[:], sq[:, :, 1], root, ALU.mult))
                    step(dve.tensor_tensor(ang[:], proj, bc(norm[:]), ALU.mult))
                    step(dve.tensor_tensor(ang[:], ang[:], brf[:].rearrange("p (a f) -> p a f", a=1).broadcast_to([P, T, RF]), ALU.add))
                    step(dve.tensor_scalar(turns[:], ang[:], 1.0 / TWO_PI, MAGIC, ALU.mult, ALU.add))
                    step(dve.tensor_scalar(turns[:], turns[:], -MAGIC, None, ALU.add))
                    for part_of_2pi in (C1, C2, C3):
                        step(dve.scalar_tensor_tensor(out=ang[:], in0=turns[:], scalar=-part_of_2pi, in1=ang[:], op0=ALU.mult, op1=ALU.add))
                    step(dve.tensor_scalar(ang[:], ang[:], -PI_IN, PI_IN, ALU.max, ALU.min))
                    dve.sem_inc(reduced, 1)
                    dve.wait_ge(tanhed, 1)
                    step(dve.memset(powers[:, :, 0], 1.0))
                    step(dve.tensor_copy(powers[:, :, 1], charge))
                    for m in range(2, NM):
                        step(dve.tensor_tensor(powers[:, :, m], powers[:, :, m - 1], charge, ALU.mult))
                    for m in range(NM):
                        step(dve.tensor_scalar(powers[:, :, m], powers[:, :, m], mags[m] * scale, None, ALU.mult))

                @block.scalar
                def _(act):
                    z, one_z, ln_z, v = (temp[:, n:n + 1] for n in (1, 2, 3, 0))
                    act.activation(z, v, ACT.Abs).then_inc(expd, 1)
                    act.wait_ge(expd, 1)
                    act.activation(z, z, ACT.Exp, scale=-1.0).then_inc(expd, 1)
                    act.wait_ge(expd, 2)
                    act.activation(one_z, z, ACT.Copy, bias=1.0).then_inc(expd, 1)
                    act.wait_ge(expd, 3)
                    act.activation(ln_z, one_z, ACT.Ln).then_inc(lnd, 1)
                    act.wait_ge(norm2, 1)
                    act.activation(sq[:, :, 0], norm[:], ACT.Sqrt).then_inc(norm_ready, 1)
                    act.activation(charge, charge, ACT.Tanh).then_inc(tanhed, 1)
                    act.wait_ge(reduced, 1)
                    act.activation(feats[:, :, RF:NF], ang[:], ACT.Sin).then_inc(sines, 1)
                    act.activation(ang[:], ang[:], ACT.Abs).then_inc(abs_done, 1)
                    act.wait_ge(abs_done, 1)
                    act.wait_ge(dve_b, 1)
                    act.activation(feats[:, :, 0:RF], ang[:], ACT.Sin, bias=half_pi[:, 0:1], scale=-1.0).then_inc(sines, 1)

        with ExitStack() as part:
            psb = lambda n, shape, dt=F32: k.sb(f"{name}_{n}", shape, dt, part)
            RL = 4
            tp, tpt = psb("tp", [P, 2, TB, NM * NF]), psb("tpt", [P, 3, BLOCK])
            phi = psb("phi", [SH, 2, SEQ])
            lg, pt = psb("lg", [P, RL, SEQ]), psb("pt", [P, 2, SEQ])
            top, den = psb("top", [P, RL]), psb("den", [P, RL])
            (tp_ready, tp_turned, tpt_ready, phi_ps, phi_ready, l_ps, l_read, top_ready, e_ready, p_turned, pt_low, pt_high,
             o_ps, den_ready, resid, stats_done, gate) = sem(
                "tp_ready tp_turned tpt_ready phi_ps phi_ready l_ps l_read top_ready e_ready p_turned pt_low pt_high "
                "o_ps den_ready resid stats_done gate")
            two = lambda b: ps[:, b:b + 2, :].rearrange("p a b -> p (a b)")
            widths = ((0, P), (P, P), (2 * P, NF))
            HALF = NT // 2
            PHI = [(0, "turn", 0, 0, 5), (0, "turn", 0, 1, 7), (1, "turn", 0, 2, 5), (2, "phi", 0, 0, 7), (2, "turn", 1, 0, 5),
                   (3, "turn", 1, 1, 7), (3, "turn", 1, 2, 5), (4, "phi", 1, 0, 7)]

            def pieces(own, b, u, i):
                for at, piece, m, c, bank in PHI:
                    if at == i and piece in own:
                        own[piece](b, u, m, c, bank)

            def all_pieces(own):
                for i in range(NT):
                    pieces(own, 0, 0, i)

            def sequences(engine, sequence):
                sequence(0, 0, True, True)
                with engine.Fori(0, NB // 2 - 1) as half:
                    sequence(half * 2 + 1, 1, False, True)
                    sequence(half * 2 + 2, 0, False, True)
                sequence(NB - 1, 1, False, False)

            with nc.Block() as block:
                @block.gpsimd
                def _(pool):
                    with pool.Fori(0, NB) as b:
                        for m in range(2):
                            i = b * 2 + m
                            pool.wait_ge(tp_turned, i * 3 + 1)
                            pool.sem_inc(gate, 1)
                            pool.tensor_tensor(tp[:, m, :, :].rearrange("p t (m f) -> p t m f", f=NF),
                                               powers[:, bass.ds(i * TB, TB), :].rearrange("p t (m a) -> p t m a", a=1).broadcast_to([P, TB, NM, NF]),
                                               feats[:, bass.ds(i * TB, TB), :].rearrange("p t (a f) -> p t a f", a=1).broadcast_to([P, TB, NM, NF]),
                                               ALU.mult).then_inc(tp_ready, 1)

                @block.vector
                def _(dve):
                    def maxed(b, i):
                        g, n = b * NT + i, (i + 1) * P
                        dve.wait_ge(l_ps, g + 2)
                        dve.wait_ge(p_turned, g + 1)
                        dve.sem_inc(gate, 1)
                        dve.tensor_tensor_reduce(out=lg[:, i % RL, 0:n], in0=two(2 * (i % 2))[:, 0:n], in1=decay[:, SEQ - n:],
                                                 scale=1.0, scalar=-BIG, op0=ALU.mult, op1=ALU.max,
                                                 accum_out=top[:, i % RL:i % RL + 1]).then_inc(l_read, 1)
                        dve.wait_ge(l_read, g + 3)
                        dve.tensor_scalar(top[:, i % RL:i % RL + 1], top[:, i % RL:i % RL + 1], -1.0, None, ALU.mult).then_inc(top_ready, 1)

                    def turned_high(b, i):
                        if i >= HALF:
                            dve.wait_ge(p_turned, b * NT + i + 1 + RL)
                            dve.wait_ge(o_ps, b * NT + i + 1)
                            dve.tensor_copy(pt[:, i % 2, BLOCK:(i + 1) * P], ps[:, 5, 0:(i + 1) * P - BLOCK]).then_inc(pt_high, 1)

                    def residual(b, i):
                        g = b * NT + i
                        dve.wait_ge(e_ready, g + 1)
                        dve.reciprocal(den[:, i % RL:i % RL + 1], den[:, i % RL:i % RL + 1]).then_inc(den_ready, 1)
                        dve.wait_ge(o_ps, g + 3)
                        dve.wait_ge(den_ready, g + 1)
                        x_tile = k.X[:, bass.ds(g, 1), :].rearrange("p a f -> p (a f)")
                        dve.scalar_tensor_tensor(out=x_tile, in0=ps[:, 6, 0:D], scalar=den[:, i % RL:i % RL + 1], in1=x_tile,
                                                 op0=ALU.mult, op1=ALU.add).then_inc(resid, 1)
                        dve.wait_ge(resid, g + 2)
                        tile_stats(k, dve, g).then_inc(stats_done, 1)

                    def keep_turned(b, u, m, c, bank):
                        at, n = widths[c]
                        dve.wait_ge(tp_turned, (b * 2 + m) * 3 + c + 5)
                        dve.wait_ge(phi_ps, b * 2 + m + 1)
                        dve.tensor_copy(tpt[0:n, c, :], ps[0:n, bank, :]).then_inc(tpt_ready, 1)

                    def sequence(b, u, first, ahead):
                        for i in range(NT):
                            if i + 1 < NT:
                                maxed(b, i + 1)
                            elif ahead:
                                maxed(b + 1, 0)
                            if ahead:
                                pieces(dict(turn=keep_turned), b + 1, 1 - u, i)
                            turned_high(b, i)
                            if i > 0:
                                residual(b, i - 1)
                            elif not first:
                                residual(b - 1, NT - 1)
                        if not ahead:
                            residual(b, NT - 1)

                    dve.sem_inc(resid, 1)
                    dve.sem_inc(l_read, 2)
                    all_pieces(dict(turn=keep_turned))
                    maxed(0, 0)
                    sequences(dve, sequence)

                @block.scalar
                def _(act):
                    def exponentials(b, i):
                        g, n = b * NT + i, (i + 1) * P
                        act.wait_ge(top_ready, g + 1)
                        act.activation(lg[:, i % RL, 0:n], lg[:, i % RL, 0:n], ACT.Exp, bias=top[:, i % RL:i % RL + 1],
                                       accum_out=den[:, i % RL:i % RL + 1]).then_inc(e_ready, 1)

                    def keep_phi(b, u, m, c, bank):
                        act.wait_ge(phi_ps, b * 2 + m + 2)
                        act.wait_ge(l_ps, b * NT + 1 - (NT if not isinstance(b, int) else min(NT, b * NT)))
                        act.activation(phi[:, u, m * BLOCK:(m + 1) * BLOCK], ps[0:SH, 7, :], ACT.Copy).then_inc(phi_ready, 1)

                    def sequence(b, u, first, ahead):
                        for i in range(NT):
                            if i + 1 < NT:
                                exponentials(b, i + 1)
                            elif ahead:
                                exponentials(b + 1, 0)
                            g, n = b * NT + i, min((i + 1) * P, BLOCK)
                            act.wait_ge(p_turned, g + 1 + RL)
                            act.wait_ge(o_ps, g + 1)
                            act.activation(pt[:, i % 2, 0:n], ps[:, 4, 0:n], ACT.Copy).then_inc(pt_low, 1)
                            if ahead:
                                pieces(dict(phi=keep_phi), b + 1, 1 - u, i)

                    act.sem_inc(phi_ready, 1)
                    all_pieces(dict(phi=keep_phi))
                    exponentials(0, 0)
                    sequences(act, sequence)

                @block.tensor
                def _(pe):
                    def logits(b, u, i):
                        g, n = b * NT + i, (i + 1) * P
                        if i == 0:
                            pe.wait_ge(phi_ready, b * 2 + 3)
                        pe.wait_ge(l_read, g + 1)
                        q = phi[:, u, i * P:(i + 1) * P]
                        for c in range(0, n, BLOCK):
                            z = min(n, c + BLOCK)
                            pe.matmul(two(2 * (i % 2))[:, c:z], q, phi[:, u, c:z], start=True, stop=z < n)
                        pe.matmul(two(2 * (i % 2))[:, i * P:n], k.ident_bf[:], mask[:], start=False, stop=True).then_inc(l_ps, 1)

                    def turn_products(b, u, m, c, bank):
                        at, n = widths[c]
                        blk = b * 2 + m
                        pe.wait_ge(tp_ready, blk + 1)
                        pe.wait_ge(phi_ready, blk + 1)
                        if c == 2:
                            pe.wait_ge(tpt_ready, blk * 3 + 1)
                        if c == 0 and m == 0:
                            pe.wait_ge(pt_high, b * HALF + 1 - (HALF if not isinstance(b, int) else min(HALF, b * HALF)))
                        pe.sem_inc(gate, 1)
                        for t in range(TB):
                            last = pe.transpose(ps[0:n, bank, t * P:(t + 1) * P], tp[:, m, t, at:at + n], k.ident[:])
                        last.then_inc(tp_turned, 1)

                    def combine(b, u, m, c, bank):
                        blk = b * 2 + m
                        pe.wait_ge(tpt_ready, blk * 3 + 3)
                        pe.sem_inc(gate, 1)
                        for c, (at, n) in enumerate(widths):
                            last = pe.matmul(ps[0:SH, 7, :], wc[0:n, c, :], tpt[0:n, c, :], start=c == 0, stop=c == 2)
                        last.then_inc(phi_ps, 1)

                    own = dict(turn=turn_products, phi=combine)

                    def turn(b, i, ahead):
                        g, n = b * NT + i, (i + 1) * P
                        pe.wait_ge(e_ready, g + 1)
                        pe.wait_ge(pt_low, g + 1)
                        if i >= HALF:
                            pe.wait_ge(pt_high, b * HALF + i - HALF + 1)
                            if ahead:
                                pe.wait_ge(tpt_ready, b * 6 + 12)
                        for c in range(i + 1):
                            last = pe.transpose(two(4)[:, c * P:(c + 1) * P], lg[:, i % RL, c * P:(c + 1) * P], k.ident[:])
                        last.then_inc(p_turned, 1)

                    def values(b, i):
                        g, n = b * NT + i, (i + 1) * P
                        pe.wait_ge(pt_low, g + 2)
                        if i >= HALF:
                            pe.wait_ge(pt_high, b * HALF + i - HALF + 2)
                        pe.wait_ge(resid, g + 1)
                        for c in range(i + 1):
                            last = pe.matmul(ps[:, 6, 0:D], pt[:, i % 2, c * P:(c + 1) * P],
                                             vw[:, bass.ds(b * NT + c, 1), :].rearrange("p a f -> p (a f)"), start=c == 0, stop=c == i)
                        last.then_inc(o_ps, 1)

                    def sequence(b, u, first, ahead):
                        for i in range(NT):
                            if i + 2 < NT:
                                logits(b, u, i + 2)
                            elif ahead:
                                logits(b + 1, 1 - u, i + 2 - NT)
                            turn(b, i, ahead)
                            if i > 0:
                                values(b, i - 1)
                            elif not first:
                                values(b - 1, NT - 1)
                            if ahead:
                                pieces(own, b + 1, 1 - u, i)
                        if not ahead:
                            values(b, NT - 1)

                    for credit, n in ((tp_turned, 4), (phi_ps, 1), (l_ps, 1), (p_turned, RL), (o_ps, 2), (pt_low, 1), (pt_high, 1)):
                        pe.sem_inc(credit, n)
                    all_pieces(own)
                    logits(0, 0, 0)
                    logits(0, 0, 1)
                    sequences(pe, sequence)


TOKENS = 8 * 1024


def program(nc, t, out, n_dram, y_dram):
    ffn0 = dict(router=t["L0_ffn_router"], sel=t["sel_weights"], em8=t["expert_less_8"], eg=t["L0_ffn_experts_gate"],
                eu=t["L0_ffn_experts_up"], ed=t["L0_ffn_experts_down"], sg=t["L0_ffn_shared_gate"],
                su=t["L0_ffn_shared_up"], sd=t["L0_ffn_shared_down"])
    scan = dict(xproj_t=t["L0_attn_xproj_w"], dt_wt=t["L0_attn_dt_w"], v_wt=t["L0_attn_v_w"], v_b=t["L0_attn_v_b"],
                norm_w=t["L0_attn_norm_w"], dt_b=t["L0_attn_dt_b"], D_p=t["L0_attn_D_p"], A_log=t["L0_attn_A_log"],
                sel_bc=t["sel_bc"])
    gated = dict(mx_wt=t["L0_attn_mx_w"], h_wt=t["L0_attn_h_w"], h_b=t["L0_attn_h_b"], rot=t["rotation"],
                 alpha=t["alpha_beta"], causal=t["causal_chunk"], gamma_t=t["L0_attn_gamma"],
                 beta_t=t["L0_attn_beta"], mx_bt=t["L0_attn_mx_b"])
    attn1 = dict(shell_t=t["L1_attn_W_shell"], charge_t=t["L1_attn_W_charge"], v=t["L1_attn_W_v"], shell=t["shell_rows"], out_t=t["L1_attn_W_out"],
                 omega_t=t["L1_attn_omega"], combine_t=t["L1_attn_W_combine"], b_shell=t["L1_attn_b_shell"],
                 b_charge=t["L1_attn_b_charge"], b_v=t["L1_attn_b_v"], b_out=t["L1_attn_b_out"],
                 rff_bias=t["L1_attn_rff_bias"], decay=t["distance_decay"], mask=t["causal_tile"], log_temp=t["L1_attn_log_temp"])
    ffn1 = dict(router_w=t["L1_ffn_router_w"], router_b=t["L1_ffn_router_b"], W1=t["L1_ffn_W1"], b1_t=t["L1_ffn_b1"],
                W2=t["L1_ffn_W2"], b2=t["L1_ffn_b2"], em8=t["expert_less_8"], before=t["before"], row_no=t["row_no"],
                trash_row=t["trash_row"], lane=t["lane"], token1=t["token1"])
    with ExitStack() as ctx:
        k = Core(nc, ctx, TOKENS)
        stage_load(k, t["L0_attn_x"], t["identity"])
        stage_ffn0(k, "ffn_a", ffn0)
        with ExitStack() as layer:
            V = k.sb("V", [P, k.tiles, D], ctx=layer)
            Y = k.sb("Y", [P, TOKENS], ctx=layer)
            stage_scan(k, "scan", scan, V, Y)
            stage_gated_attention(k, "gated", gated, V, Y)
        k.clear_semaphores()
        stage_ffn0(k, "ffn_b", ffn0)
        stage_expert_ffn(k, "ffn_c", ffn1, n_dram, y_dram)
        k.clear_semaphores()
        stage_kernel_attention(k, "attn", attn1)
        stage_expert_ffn(k, "ffn_d", ffn1, n_dram, y_dram)
        stage_store(k, out)



def shape_constants():
    import math
    f, bf = np.float32, mybir.dt.np(BF16)
    p = np.arange(P)[:, None]
    tiles = TOKENS // P
    sel = np.zeros((P, TB * 4, P), bf)
    for c in range(TB):
        for j in range(4):
            for part in range(3):
                for e in range(2):
                    sel[32 * c + part * 8 + 2 * j + e, c * 4 + j, e * 64:(e + 1) * 64] = 1
    sel_bc = np.zeros((96, 32, P), bf)
    for part in range(3):
        for n in range(32):
            sel_bc[part * 32 + n, n, :] = 1
    freqs = np.exp(np.arange(64, dtype=f) * f(-math.log(10000.0) / 64)).astype(f)
    ang = (np.arange(256, dtype=f)[:, None] * freqs[None]).astype(f)
    cos, sin = np.cos(ang).T, np.sin(ang).T
    rotation = np.concatenate([np.concatenate([cos, cos], 0), np.concatenate([-sin, sin], 0)], 1).astype(f)
    key = np.arange(256)[None]
    causal_chunk = np.concatenate([np.where(key > t * P + p, -BIG, 0.0) for t in range(2)], 1).astype(f)
    return dict(identity=np.eye(P, dtype=f), sel_weights=sel.reshape(P, -1), sel_bc=sel_bc.reshape(96, -1),
                expert_less_8=np.tile(np.arange(8, dtype=f) - 8, (P, tiles)), rotation=rotation, causal_chunk=causal_chunk,
                distance_decay=np.exp(-0.03 * np.abs(p - np.arange(1024)[None] + 896)).astype(f),
                causal_tile=np.where(np.arange(P)[None] > p, -BIG, 0.0).astype(bf),
                before=(p < np.arange(P)[None]).astype(bf),
                row_no=np.tile(np.arange(tiles + 8, dtype=f), (P, 1)),
                trash_row=(TOKENS + 1 + P * np.arange(tiles + 8)[None] + p).astype(f),
                lane=np.tile(np.arange(P, dtype=f), (P, 1)),
                token1=(P * np.arange(tiles)[None] + p + 1).astype(f))


def kernel(**inputs):
    import concourse.bacc as bacc
    from concourse.bass_utils import run_bass_kernel_spmd

    laid = {name: np.asarray(a) for name, a in inputs.items()}
    laid["shell_rows"] = laid["L1_attn_W_shell"]
    laid["L0_attn_x"] = laid["L0_attn_x"].reshape(TOKENS, D)
    for name in ("L0_attn_xproj_w", "L0_attn_dt_w", "L0_attn_v_w", "L0_attn_mx_w", "L0_attn_h_w", "L0_attn_gamma", "L0_attn_beta",
                 "L1_attn_W_shell", "L1_attn_W_charge", "L1_attn_W_out", "L1_attn_omega", "L1_attn_W_combine"):
        laid[name] = laid[name].T
    laid["L0_attn_mx_b"] = laid["L0_attn_mx_b"].reshape(4, D).T
    laid["L1_attn_log_temp"] = laid["L1_attn_log_temp"].reshape(1)
    laid["L1_ffn_b1"] = laid["L1_ffn_b1"].reshape(8, 4, P).transpose(2, 0, 1)
    alpha, beta = laid.pop("L0_attn_alpha_rb")[0], laid.pop("L0_attn_beta_rb")[0]
    laid["alpha_beta"] = np.stack([alpha, np.roll(alpha, 64), beta, np.roll(beta, 64)], 1)
    laid.update(shape_constants())

    nc = bacc.Bacc("TRN2", target_bir_lowering=False, num_devices=1)
    arrays, tensors = {}, {}
    for name, a in laid.items():
        arrays[f"in_{name}"] = a = np.ascontiguousarray(a)
        tensors[name] = nc.dram_tensor(f"in_{name}", a.shape, mybir.dt.from_np(a.dtype), kind="ExternalInput").ap()
    out = nc.dram_tensor("out_x", (TOKENS, D), F32, kind="ExternalOutput").ap()
    n_dram = nc.dram_tensor("normalised_rows", (TOKENS, D), F32).ap()
    y_dram = nc.dram_tensor("expert_rows", (TOKENS + (TOKENS // P + 8) * P, D), F32).ap()
    program(nc, tensors, out, n_dram, y_dram)
    r = run_bass_kernel_spmd(nc, [arrays], core_ids=[0])
    return r.results[0]["out_x"].reshape(8, 1024, D)
```
